# Optimizing a Trainium2 kernel written in Bass

```python
import numpy as np
import jax
import jax.numpy as jnp

def _softmax(x, axis=-1):
    return jax.nn.softmax(x, axis=axis)

def _gelu(x):
    return jax.nn.gelu(x, approximate=True)

def _silu(x):
    return jax.nn.silu(x)

def _sigmoid(x):
    return jax.nn.sigmoid(x)

def _layernorm(x, axis=-1, eps=1e-05):
    m = jnp.mean(x, axis=axis, keepdims=True)
    v = jnp.var(x, axis=axis, keepdims=True)
    return (x - m) / jnp.sqrt(v + eps)

def _scatter_add(tgt, idx, src, axis=0):
    return tgt.at[idx].add(src)

def _segment_sum(src, seg, n):
    return jax.ops.segment_sum(src, seg, n)
kernel_name = 'mk_gnn_preln_d4_gnn_r32_7fdc14'

def setup_inputs(seed: int=0):
    np.random.seed(seed)
    _w = jnp.asarray

    def _rec_inputs():
        import jax
        import jax.numpy as jnp
        _gk = jax.random.key(seed)
        x = -0.000202 + 1 * jax.random.normal(jax.random.fold_in(_gk, 1), (3125, 128), jnp.float32)
        _s = jax.random.randint(jax.random.fold_in(_gk, 2), (25000,), 0, 3125, jnp.int32)
        _d = jax.random.randint(jax.random.fold_in(_gk, 3), (25000,), 0, 3125, jnp.int32)
        _loop = jnp.arange(3125, dtype=jnp.int32)
        src = jnp.concatenate([_s, _d, _loop])
        dst = jnp.concatenate([_d, _s, _loop])
        _o = jnp.argsort(dst, stable=True)
        src = src[_o]
        dst = dst[_o]
        edge_type_8 = jax.random.randint(jax.random.fold_in(_gk, 13), (53125,), 0, 8, jnp.int32)
        edge_weight = jax.random.uniform(jax.random.fold_in(_gk, 14), (53125,), jnp.float32, 0.0, 1)
        return (x, src, dst, edge_type_8, edge_weight)
    x, src, dst, edge_type_8, edge_weight = _rec_inputs()

    def _L0_gnn_setup():
        import jax, jax.numpy as jnp
        import numpy as np
        NEG_SLOPE = 0.2
        key = jax.random.key(seed)
        k = jax.random.split(key, 6)
        N, E, D, H = (50000, 25000, 128, 128)
        x = jax.random.normal(k[0], (N, D), dtype=jnp.float32)
        edge_index = jax.random.randint(k[1], (2, E), 0, N, dtype=jnp.int32)
        W1 = jax.random.normal(k[2], (H, D), dtype=jnp.float32) * (1.0 / np.sqrt(D))
        W2 = jax.random.normal(k[3], (H, D), dtype=jnp.float32) * (1.0 / np.sqrt(D))
        a_s = jax.random.normal(k[4], (H,), dtype=jnp.float32) * 0.1
        a_t = jax.random.normal(k[5], (H,), dtype=jnp.float32) * 0.1
        return {'x': x, 'edge_index': edge_index, 'W1': W1, 'W2': W2, 'a_s': a_s, 'a_t': a_t}
    _L0_gnn_all = _L0_gnn_setup()
    _L0_gnn_in = {k: v for k, v in _L0_gnn_all.items() if k in ('W1', 'W2', 'a_s', 'a_t')}
    del _L0_gnn_all

    def _L1_gnn_setup():
        import jax, jax.numpy as jnp
        import numpy as np
        N_NODES = 3125
        N_EDGES = 18750
        IN_FEAT = 128
        OUT_FEAT = 128
        NUM_RELS = 8
        NUM_BASES = 4
        key = jax.random.key(seed)
        ks = jax.random.split(key, 8)
        h = jax.random.normal(ks[0], (N_NODES, IN_FEAT), dtype=jnp.float32)
        weight = jax.random.normal(ks[1], (NUM_BASES, IN_FEAT, OUT_FEAT), dtype=jnp.float32) * (1.0 / np.sqrt(IN_FEAT))
        w_comp = jax.random.normal(ks[2], (NUM_RELS, NUM_BASES), dtype=jnp.float32) * (1.0 / np.sqrt(NUM_BASES))
        root_weight = jax.random.normal(ks[3], (IN_FEAT, OUT_FEAT), dtype=jnp.float32) * (1.0 / np.sqrt(IN_FEAT))
        bias = jnp.zeros((OUT_FEAT,), dtype=jnp.float32)
        src = jax.random.randint(ks[4], (N_EDGES,), 0, N_NODES, dtype=jnp.int32)
        dst = jax.random.randint(ks[5], (N_EDGES,), 0, N_NODES, dtype=jnp.int32)
        rel_type = jax.random.randint(ks[6], (N_EDGES,), 0, NUM_RELS, dtype=jnp.int32)
        return {'h': h, 'weight': weight, 'w_comp': w_comp, 'root_weight': root_weight, 'bias': bias, 'src': src, 'dst': dst, 'rel_type': rel_type}
    _L1_gnn_all = _L1_gnn_setup()
    _L1_gnn_in = {k: v for k, v in _L1_gnn_all.items() if k in ('weight', 'w_comp', 'root_weight', 'bias')}
    del _L1_gnn_all

    def _L2_gnn_setup():
        import jax, jax.numpy as jnp
        import numpy as np
        N = 3125
        E = 20000
        DIN = 128
        DMID = 128
        EPS = 1e-05

        def gcn_conv(x, src, dst, W, b, n_nodes):
            h = x @ W.T
            ones = jnp.ones(src.shape[0], dtype=x.dtype)
            deg = jax.ops.segment_sum(ones, dst, num_segments=n_nodes)
            dinv = jnp.where(deg > 0, jax.lax.rsqrt(deg), 0.0)
            norm = dinv[src] * dinv[dst]
            msg = h[src] * norm[:, None]
            out = jax.ops.segment_sum(msg, dst, num_segments=n_nodes)
            return out + b

        def graph_layernorm(x, gamma, beta):
            mean = jnp.mean(x)
            xc = x - mean
            var = jnp.mean(xc * xc)
            return xc * jax.lax.rsqrt(var + EPS) * gamma + beta
        key = jax.random.key(seed)
        ks = jax.random.split(key, 8)
        x = jax.random.normal(ks[0], (N, DIN), dtype=jnp.float32)
        edge_index = jax.random.randint(ks[1], (2, E), 0, N, dtype=jnp.int64)
        s1 = 1.0 / np.sqrt(DIN)
        s2 = 1.0 / np.sqrt(DMID)
        W1 = jax.random.uniform(ks[2], (DMID, DIN), jnp.float32, -s1, s1)
        b1 = jnp.zeros((DMID,), jnp.float32)
        g1 = jnp.ones((DMID,), jnp.float32)
        be1 = jnp.zeros((DMID,), jnp.float32)
        W2 = jax.random.uniform(ks[3], (DMID, DMID), jnp.float32, -s2, s2)
        b2 = jnp.zeros((DMID,), jnp.float32)
        g2 = jnp.ones((DMID,), jnp.float32)
        be2 = jnp.zeros((DMID,), jnp.float32)
        return {'x': x, 'edge_index': edge_index, 'W1': W1, 'b1': b1, 'g1': g1, 'be1': be1, 'W2': W2, 'b2': b2, 'g2': g2, 'be2': be2}
    _L2_gnn_all = _L2_gnn_setup()
    _L2_gnn_in = {k: v for k, v in _L2_gnn_all.items() if k in ('W1', 'b1', 'g1', 'be1', 'W2', 'b2', 'g2', 'be2')}
    del _L2_gnn_all

    def _L3_gnn_setup():
        import jax, jax.numpy as jnp
        import numpy as np
        N, E, IN_DIM, OUT_DIM, HEADS = (50000, 25000, 128, 32, 4)

        def _linear_params(key, fan_in, fan_out, bias=True):
            kw, kb = jax.random.split(key)
            s = 1.0 / np.sqrt(fan_in)
            W = jax.random.uniform(kw, (fan_in, fan_out), jnp.float32, -s, s)
            b = jax.random.uniform(kb, (fan_out,), jnp.float32, -s, s) if bias else None
            return (W, b)

        def _transformer_conv(x, src, dst, ea, Wq, bq, Wk, bk, Wv, bv, We, Ws, bs, H, C):
            n = x.shape[0]
            q = (x @ Wq + bq).reshape(n, H, C)
            k = (x @ Wk + bk).reshape(n, H, C)
            v = (x @ Wv + bv).reshape(n, H, C)
            e = (ea @ We).reshape(-1, H, C)
            kj = k[src] + e
            vj = v[src] + e
            alpha = jnp.einsum('ehc,ehc->eh', q[dst], kj) / jnp.sqrt(jnp.asarray(C, x.dtype))
            amax = jax.ops.segment_max(alpha, dst, num_segments=n)
            p = jnp.exp(alpha - amax[dst])
            denom = jax.ops.segment_sum(p, dst, num_segments=n)
            w = p / denom[dst]
            msg = (vj * w[..., None]).reshape(-1, H * C)
            out = jax.ops.segment_sum(msg, dst, num_segments=n)
            return out + x @ Ws + bs
        key = jax.random.key(seed)
        ks = jax.random.split(key, 24)
        H, C = (HEADS, OUT_DIM)
        inp = {'x': jax.random.normal(ks[0], (N, IN_DIM), jnp.float32), 'edge_weight': jax.random.uniform(ks[1], (E,), jnp.float32)}
        for li, fan_in in ((1, IN_DIM), (2, H * C)):
            base = 2 + (li - 1) * 10
            inp[f'Wq{li}'], inp[f'bq{li}'] = _linear_params(ks[base + 0], fan_in, H * C)
            inp[f'Wk{li}'], inp[f'bk{li}'] = _linear_params(ks[base + 1], fan_in, H * C)
            inp[f'Wv{li}'], inp[f'bv{li}'] = _linear_params(ks[base + 2], fan_in, H * C)
            We, _ = _linear_params(ks[base + 3], 1, H * C, bias=False)
            inp[f'We{li}'] = We
            inp[f'Ws{li}'], inp[f'bs{li}'] = _linear_params(ks[base + 4], fan_in, H * C)
        inp['edge_index'] = jax.random.randint(ks[22], (2, E), 0, N, jnp.int64)
        return inp
    _L3_gnn_all = _L3_gnn_setup()
    _L3_gnn_in = {k: v for k, v in _L3_gnn_all.items() if k in ('Wq1', 'bq1', 'Wk1', 'bk1', 'Wv1', 'bv1', 'We1', 'Ws1', 'bs1', 'Wq2', 'bq2', 'Wk2', 'bk2', 'Wv2', 'bv2', 'We2', 'Ws2', 'bs2')}
    del _L3_gnn_all
    return {'x': x, 'src': src, 'dst': dst, 'edge_type_8': edge_type_8, 'edge_weight': edge_weight, 'L0_gnn_W1': _L0_gnn_in['W1'], 'L0_gnn_W2': _L0_gnn_in['W2'], 'L0_gnn_a_s': _L0_gnn_in['a_s'], 'L0_gnn_a_t': _L0_gnn_in['a_t'], 'L1_gnn_weight': _L1_gnn_in['weight'], 'L1_gnn_w_comp': _L1_gnn_in['w_comp'], 'L1_gnn_root_weight': _L1_gnn_in['root_weight'], 'L1_gnn_bias': _L1_gnn_in['bias'], 'L2_gnn_W1': _L2_gnn_in['W1'], 'L2_gnn_b1': _L2_gnn_in['b1'], 'L2_gnn_g1': _L2_gnn_in['g1'], 'L2_gnn_be1': _L2_gnn_in['be1'], 'L2_gnn_W2': _L2_gnn_in['W2'], 'L2_gnn_b2': _L2_gnn_in['b2'], 'L2_gnn_g2': _L2_gnn_in['g2'], 'L2_gnn_be2': _L2_gnn_in['be2'], 'L3_gnn_Wq1': _L3_gnn_in['Wq1'], 'L3_gnn_bq1': _L3_gnn_in['bq1'], 'L3_gnn_Wk1': _L3_gnn_in['Wk1'], 'L3_gnn_bk1': _L3_gnn_in['bk1'], 'L3_gnn_Wv1': _L3_gnn_in['Wv1'], 'L3_gnn_bv1': _L3_gnn_in['bv1'], 'L3_gnn_We1': _L3_gnn_in['We1'], 'L3_gnn_Ws1': _L3_gnn_in['Ws1'], 'L3_gnn_bs1': _L3_gnn_in['bs1'], 'L3_gnn_Wq2': _L3_gnn_in['Wq2'], 'L3_gnn_bq2': _L3_gnn_in['bq2'], 'L3_gnn_Wk2': _L3_gnn_in['Wk2'], 'L3_gnn_bk2': _L3_gnn_in['bk2'], 'L3_gnn_Wv2': _L3_gnn_in['Wv2'], 'L3_gnn_bv2': _L3_gnn_in['bv2'], 'L3_gnn_We2': _L3_gnn_in['We2'], 'L3_gnn_Ws2': _L3_gnn_in['Ws2'], 'L3_gnn_bs2': _L3_gnn_in['bs2']}

def reference(x, src, dst, edge_type_8, edge_weight, L0_gnn_W1, L0_gnn_W2, L0_gnn_a_s, L0_gnn_a_t, L1_gnn_weight, L1_gnn_w_comp, L1_gnn_root_weight, L1_gnn_bias, L2_gnn_W1, L2_gnn_b1, L2_gnn_g1, L2_gnn_be1, L2_gnn_W2, L2_gnn_b2, L2_gnn_g2, L2_gnn_be2, L3_gnn_Wq1, L3_gnn_bq1, L3_gnn_Wk1, L3_gnn_bk1, L3_gnn_Wv1, L3_gnn_bv1, L3_gnn_We1, L3_gnn_Ws1, L3_gnn_bs1, L3_gnn_Wq2, L3_gnn_bq2, L3_gnn_Wk2, L3_gnn_bk2, L3_gnn_Wv2, L3_gnn_bv2, L3_gnn_We2, L3_gnn_Ws2, L3_gnn_bs2):
    import jax
    import jax.numpy as jnp

    def _L0_gnn_ref(x, edge_index, W1, W2, a_s, a_t):
        import jax, jax.numpy as jnp
        import numpy as np
        NEG_SLOPE = 0.2
        N = x.shape[0]
        loop = jnp.arange(N, dtype=edge_index.dtype)
        src = jnp.concatenate([edge_index[0], loop])
        tgt = jnp.concatenate([edge_index[1], loop])
        wx_src = x @ W1.T
        wx_tgt = x @ W2.T
        s_i = wx_tgt @ a_s
        s_j = wx_src @ a_t
        e = jax.nn.leaky_relu(s_i[tgt] + s_j[src], negative_slope=NEG_SLOPE)
        m = jax.ops.segment_max(e, tgt, num_segments=N)
        ex = jnp.exp(e - m[tgt])
        denom = jax.ops.segment_sum(ex, tgt, num_segments=N)
        alpha = ex / denom[tgt]
        out = jax.ops.segment_sum(wx_src[src] * alpha[:, None], tgt, num_segments=N)
        return out

    def _L1_gnn_ref(h, weight, w_comp, root_weight, bias, src, dst, rel_type):
        import jax, jax.numpy as jnp
        import numpy as np
        N_NODES = 3125
        N_EDGES = 18750
        IN_FEAT = 128
        OUT_FEAT = 128
        NUM_RELS = 8
        NUM_BASES = 4
        B, I, O = weight.shape
        R = w_comp.shape[0]
        W = (w_comp @ weight.reshape(B, I * O)).reshape(R, I, O)
        proj = jnp.einsum('ni,rio->nro', h, W)
        msg = proj[src, rel_type]
        agg = jax.ops.segment_sum(msg, dst, num_segments=h.shape[0])
        out = h @ root_weight + agg + bias
        return jax.nn.relu(out)

    def _L2_gnn_ref(x, edge_index, W1, b1, g1, be1, W2, b2, g2, be2):
        import jax, jax.numpy as jnp
        import numpy as np
        N = 3125
        E = 20000
        DIN = 128
        DMID = 128
        EPS = 1e-05

        def gcn_conv(x, src, dst, W, b, n_nodes):
            h = x @ W.T
            ones = jnp.ones(src.shape[0], dtype=x.dtype)
            deg = jax.ops.segment_sum(ones, dst, num_segments=n_nodes)
            dinv = jnp.where(deg > 0, jax.lax.rsqrt(deg), 0.0)
            norm = dinv[src] * dinv[dst]
            msg = h[src] * norm[:, None]
            out = jax.ops.segment_sum(msg, dst, num_segments=n_nodes)
            return out + b

        def graph_layernorm(x, gamma, beta):
            mean = jnp.mean(x)
            xc = x - mean
            var = jnp.mean(xc * xc)
            return xc * jax.lax.rsqrt(var + EPS) * gamma + beta
        n = x.shape[0]
        loops = jnp.arange(n, dtype=edge_index.dtype)
        src = jnp.concatenate([edge_index[0], loops])
        dst = jnp.concatenate([edge_index[1], loops])
        h = gcn_conv(x, src, dst, W1, b1, n)
        h = jax.nn.relu(graph_layernorm(h, g1, be1))
        h = gcn_conv(h, src, dst, W2, b2, n)
        return jax.nn.relu(graph_layernorm(h, g2, be2))

    def _L3_gnn_ref(x, edge_weight, Wq1, bq1, Wk1, bk1, Wv1, bv1, We1, Ws1, bs1, Wq2, bq2, Wk2, bk2, Wv2, bv2, We2, Ws2, bs2, edge_index):
        import jax, jax.numpy as jnp
        import numpy as np
        N, E, IN_DIM, OUT_DIM, HEADS = (50000, 25000, 128, 32, 4)

        def _linear_params(key, fan_in, fan_out, bias=True):
            kw, kb = jax.random.split(key)
            s = 1.0 / np.sqrt(fan_in)
            W = jax.random.uniform(kw, (fan_in, fan_out), jnp.float32, -s, s)
            b = jax.random.uniform(kb, (fan_out,), jnp.float32, -s, s) if bias else None
            return (W, b)

        def _transformer_conv(x, src, dst, ea, Wq, bq, Wk, bk, Wv, bv, We, Ws, bs, H, C):
            n = x.shape[0]
            q = (x @ Wq + bq).reshape(n, H, C)
            k = (x @ Wk + bk).reshape(n, H, C)
            v = (x @ Wv + bv).reshape(n, H, C)
            e = (ea @ We).reshape(-1, H, C)
            kj = k[src] + e
            vj = v[src] + e
            alpha = jnp.einsum('ehc,ehc->eh', q[dst], kj) / jnp.sqrt(jnp.asarray(C, x.dtype))
            amax = jax.ops.segment_max(alpha, dst, num_segments=n)
            p = jnp.exp(alpha - amax[dst])
            denom = jax.ops.segment_sum(p, dst, num_segments=n)
            w = p / denom[dst]
            msg = (vj * w[..., None]).reshape(-1, H * C)
            out = jax.ops.segment_sum(msg, dst, num_segments=n)
            return out + x @ Ws + bs
        src, dst = (edge_index[0], edge_index[1])
        ea = edge_weight[:, None]
        h = _transformer_conv(x, src, dst, ea, Wq1, bq1, Wk1, bk1, Wv1, bv1, We1, Ws1, bs1, HEADS, OUT_DIM)
        out = _transformer_conv(h, src, dst, ea, Wq2, bq2, Wk2, bk2, Wv2, bv2, We2, Ws2, bs2, HEADS, OUT_DIM)
        return out
    edge_index = jnp.stack([src, dst])
    h = jnp.maximum(_layernorm(x, axis=-1), 0.0)
    x = x + _L0_gnn_ref(h, edge_index, L0_gnn_W1, L0_gnn_W2, L0_gnn_a_s, L0_gnn_a_t)
    h = jnp.maximum(_layernorm(x, axis=-1), 0.0)
    x = x + _L1_gnn_ref(h, L1_gnn_weight, L1_gnn_w_comp, L1_gnn_root_weight, L1_gnn_bias, src, dst, edge_type_8)
    h = jnp.maximum(_layernorm(x, axis=-1), 0.0)
    x = x + _L2_gnn_ref(h, edge_index, L2_gnn_W1, L2_gnn_b1, L2_gnn_g1, L2_gnn_be1, L2_gnn_W2, L2_gnn_b2, L2_gnn_g2, L2_gnn_be2)
    h = jnp.maximum(_layernorm(x, axis=-1), 0.0)
    x = x + _L3_gnn_ref(h, edge_weight, L3_gnn_Wq1, L3_gnn_bq1, L3_gnn_Wk1, L3_gnn_bk1, L3_gnn_Wv1, L3_gnn_bv1, L3_gnn_We1, L3_gnn_Ws1, L3_gnn_bs1, L3_gnn_Wq2, L3_gnn_bq2, L3_gnn_Wk2, L3_gnn_bk2, L3_gnn_Wv2, L3_gnn_bv2, L3_gnn_We2, L3_gnn_Ws2, L3_gnn_bs2, edge_index)
    return x

_drawn_inputs = setup_inputs


def setup_inputs(seed=0):
    import zlib

    import numpy as np

    out = dict(_drawn_inputs(seed))
    spreads = {'L1_gnn_bias': (0.0, 0.296),
     'L2_gnn_b1': (0.0, 0.1),
     'L2_gnn_g1': (1.0, 0.2),
     'L2_gnn_be1': (0.0, 0.272),
     'L2_gnn_b2': (0.0, 0.1),
     'L2_gnn_g2': (1.0, 0.2),
     'L2_gnn_be2': (0.0, 0.29)}
    factors = {'edge_weight': 3.007,
     'L0_gnn_W2': 5.645,
     'L3_gnn_Wq1': 8.0,
     'L3_gnn_bq1': 8.0,
     'L3_gnn_Wk1': 8.0,
     'L3_gnn_bk1': 8.0,
     'L3_gnn_bv1': 3.476,
     'L3_gnn_bs1': 3.751,
     'L3_gnn_Wq2': 8.0,
     'L3_gnn_bq2': 8.0,
     'L3_gnn_Wk2': 8.0,
     'L3_gnn_bk2': 8.0,
     'L3_gnn_bv2': 2.726,
     'L3_gnn_bs2': 2.896}
    for name, (base, spread) in spreads.items():
        noise = np.random.default_rng([zlib.crc32(name.encode()), seed]).standard_normal(out[name].shape)
        drawn = base * np.exp(spread * noise) if base else spread * noise
        out[name] = jnp.asarray(drawn.astype(out[name].dtype))
    for name, factor in factors.items():
        out[name] = (out[name] * factor).astype(out[name].dtype)
    return out
```

```python
import concourse.bass as bass
from concourse import mybir
from contextlib import ExitStack


class Tally:

    def __init__(self, sem):
        self.sem, self.n, self.at = sem, 0, None

    def enter(self, i, per):
        self.at = (i, per, self.n)

    def leave(self, trips):
        _, per, start = self.at
        self.n, self.at = start + per * trips, None

    def leave_iteration(self):
        assert self.n - self.at[2] == self.at[1], (self.n - self.at[2], self.at[1])

    def step(self, instruction):
        instruction.then_inc(self.sem, 1)
        self.n += 1
        return self.value()

    def value(self):
        return self.n if self.at is None else self.at[0] * self.at[1] + self.n


def gnn_stack_kernel(nc, A, out):
    f32, bf16, i32, u32 = mybir.dt.float32, mybir.dt.bfloat16, mybir.dt.int32, mybir.dt.uint32
    ALU, ACT, AX = mybir.AluOpType, mybir.ActivationFunctionType, mybir.AxisListType
    ds = bass.ds

    N, D = A["x"].shape
    E = A["src"].shape[0]
    P = 128
    TPG, GPC = 4, 8
    TPC = TPG * GPC
    NCH = -(-E // (P * TPC))
    T = NCH * TPC
    EP = T * P
    NB = 2 * -(-(N + P) // (2 * P))
    NP = NB * P
    NPAIR = NB // 2
    NG = NCH * GPC
    FREE = GPC
    ONE = 1
    HEADS, HD = 4, D // 4
    NREL, NBASE = A["L1_gnn_w_comp"].shape
    BIG = 1e30
    EPS = 1e-5
    LASTROWS = N - (N // P) * P
    FULLB = N // P
    assert NCH * TPC * P - E < P and TPC * HEADS == P

    ctx = ExitStack()
    with ctx:
        ctx.enter_context(nc.allow_non_contiguous_dma(reason="columns of a few vectors, and one value for each window"))

        def sb(name, shape, dt=f32):
            return ctx.enter_context(nc.sbuf_tensor(name, shape, dt))

        def sem(name):
            return ctx.enter_context(nc.semaphore(name))

        def dram(name, shape, dt=f32):
            return nc.dram_tensor(name, shape, dt).ap()

        dpad = dram("dst_padded", (EP + 2,), i32)
        drow = dram("dst_in_window", (EP,), bf16)
        penrow_d = dram("open_tiles", (2, NCH, TPC), bf16)
        att0_d = dram("gat_rows", (NP, 132))
        rel_d = dram("relation_rows", (NP * NREL, D))
        gcn_d = dram("gcn_rows", (NP, D))
        kv_d = dram("key_value_rows", (NP, 2 * D))
        q0_d = dram("gat_target_scores", (NP, 4))
        q_d = dram("query_rows", (NP, 132))

        xN = sb("x_rows", [P, NB, D])
        hT = sb("h_transposed", [P, NP])
        numT = sb("sums_transposed", [P, NP])
        extT = sb("extra_sums_transposed", [8, NP])
        ring = sb("gathered_rows", [P, TPC * 2 * D])
        vbuf = sb("kept_values", [P, TPC * 132])
        ident = sb("identity", [P, P])
        iota_j = sb("iota_window", [P, P])
        neg_iota_p = sb("minus_partition", [P, 1])
        ones_row = sb("ones_row", [1, P])
        dstP = sb("dst_in_window_by_edge", [P, T])
        startP = sb("segment_start_by_edge", [P, T])
        ewP = sb("edge_weight_by_edge", [P, T])
        srcI = sb("src_index", [P, T + TPC], i32)
        relI = sb("src_relation_index", [P, T + TPC], i32)
        idx_slot = sb("index_slot", [P, TPC], i32)
        fpen = sb("start_penalty", [P, NCH, P], bf16)
        bpen = sb("end_penalty_reversed", [P, NCH, P], bf16)
        prefF = sb("start_seen_penalty", [P, NCH, P], bf16)
        prefB = sb("end_ahead_penalty", [P, NCH, P], bf16)
        penF_row = sb("tile_penalty_forward", [1, NCH, HEADS, TPC + 1], bf16)
        penB_row = sb("tile_penalty_backward_reversed", [1, NCH, HEADS, TPC], bf16)
        cont_row = sb("chunk_continues", [1, NCH])
        baseI = sb("window_base", [1, NCH * GPC], i32)
        nbI = sb("shared_node", [1, NCH], i32)
        Sb = sb("edge_node_onehot", [P, GPC, TPG, P])
        prod = sb("query_key_products", [P, 2, TPG * D])
        msg = sb("messages", [P, 2, TPG, D])
        STa = sb("window_distance", [P, 2, TPG * P], bf16)
        ST = sb("node_edge_onehot", [P, 2, TPG * P])
        drow_sb = sb("dst_in_window_row", [P, 2, (GPC // 2) * TPG * P], bf16)
        qwin = sb("query_window", [P, GPC, 132])
        alpha = sb("scores", [P, HEADS, TPC])
        alphax = sb("scan_scores", [P, HEADS, TPC])
        qwe = sb("query_edge_term", [P, HEADS, TPC])
        am = sb("scores_below_max", [P, HEADS, TPC])
        pe8 = sb("edge_factors", [P, 8, TPC])
        Fs = sb("forward_max", [P, P])
        Bs = sb("backward_max", [P, P])
        Ms = sb("segment_max", [P, P])
        M2s = sb("segment_max_backward", [P, P])
        rin = sb("tile_last_max", [1, HEADS, TPC + 1])
        SF = sb("tile_forward_max", [1, HEADS, TPC + 1])
        before_row = sb("max_before_tile", [1, P])
        after_row = sb("max_after_tile", [1, P])
        delta = sb("max_change", [1, 2, HEADS])
        delta_feat = sb("max_change_by_feature", [1, P])
        delta_ext3 = sb("max_change_by_extra", [1, 8])
        delta_ext0 = sb("max_change_by_gat_extra", [1, 4])
        facs = sb("rescale_factors", [P, 2])
        hrow = sb("normed_block", [P, 2, D])
        blkT = sb("transposed_block", [P, 2, P])
        numblk = sb("sums_block", [P, 2, P])
        extblk = sb("extra_block", [8, 2, P])
        stats = sb("norm_stats", [P, NB, 6])
        mv = sb("mean_variance", [P, NB, 2])
        rstd = sb("inverse_deviation", [P, NB])
        nbias = sb("minus_mean_scaled", [P, NB])
        eps_t = sb("epsilon", [P, 1])
        dinvN = sb("inverse_root_degree", [P, NB])
        exN = sb("extra_by_node", [P, NB, 8])
        exN2 = sb("extra_by_node_work", [P, NB, 8])
        tmpA = sb("block_work", [P, 2, D])
        R0 = sb("gat_weights", [P, 132])
        acol = sb("gat_vectors", [P, 2])
        Wr = sb("relation_weights", [P, NREL, D])
        rootW = sb("root_weight", [P, D])
        G1T = sb("gcn_w1_transposed", [P, P])
        G2T = sb("gcn_w2_transposed", [P, P])
        gcol = sb("gcn_columns", [P, 6])
        brow = sb("bias_rows", [1, 3, D])
        Rq = [sb(f"query_key_value_weights_{i}", [P, 388]) for i in range(2)]
        bq = [sb(f"query_key_value_bias_{i}", [1, 388]) for i in range(2)]
        Wsk = [sb(f"skip_weight_{i}", [P, D]) for i in range(2)]
        WeH8 = [sb(f"edge_weight_by_head_{i}", [P, 8]) for i in range(2)]
        WeH8T = [sb(f"edge_weight_by_head_row_{i}", [8, D]) for i in range(2)]
        wecol = sb("edge_weight_columns", [P, 4])
        small = sb("gcn_small", [P, 16])
        pads_sb = sb("pads", [1, 1 + P], i32)
        iota_pi = sb("partition_int", [P, 1], i32)
        ones_f = sb("ones", [P, P])
        headmask = sb("head_mask", [P, HEADS])
        sel_deg = sb("degree_row_selector", [8, P])
        done_mark = sb("done_mark", [1, 1])
        sbrow = sb("tile_backward_row", [1, P])
        wcomp = sb("relation_coefficients", [P, NREL * NBASE])
        blk2 = sb("transposed_block_next", [P, 2, P])

        ring4 = ring[:].rearrange("p (t w) -> p t w", w=2 * D)
        stage = Sb[:].rearrange("p g t j -> p (g t j)")
        stage2 = [stage[:, 0:1024], stage[:, 1024:2048]]
        hdT = vbuf[:, 0:NP]
        dinvT = ring[:, TPC * D:TPC * D + NP]
        W1nat, W2nat, g1nat, g2nat = (prod[:, 0, m * D:(m + 1) * D] for m in range(4))
        basisW = prod[:, 1, :].rearrange("p (b d) -> p b d", d=D)
        wqT = ST[:, 0, 0:2 * P].rearrange("p (q d) -> p q d", d=P)
        iota_i = numblk[:, 0, :].bitcast(i32)

        dst3 = [ring[:, j * NCH * P:(j + 1) * NCH * P].rearrange("q (c p) -> q c p", p=P) for j in range(3)]
        base_col = ring[0:TPC, 3 * NCH * P:3 * NCH * P + NCH]
        penB_in = ring[0:1, 3 * NCH * P + P:3 * NCH * P + P + NCH * P // 2].bitcast(bf16).rearrange("q (c h t) -> q c h t", h=HEADS, t=TPC)
        src_in = vbuf[0:TPC, 0:NCH * P].rearrange("q (c p) -> q c p", p=P)
        type_in = vbuf[0:TPC, NCH * P:2 * NCH * P].rearrange("q (c p) -> q c p", p=P)
        ew_in = numT[0:TPC, 0:NCH * P].rearrange("q (c p) -> q c p", p=P)
        dst_rel = numT[0:TPC, NCH * P:2 * NCH * P].rearrange("q (c p) -> q c p", p=P)
        drow_out = msg[0:TPC].rearrange("p a t d -> p (a t d)").bitcast(bf16)[:, 0:NCH * P].rearrange("q (c p) -> q c p", p=P)
        wx = hT[:].rearrange("p (b d) -> p b d", d=D)

        QX = [ctx.enter_context(nc.psum_tensor(f"QX{i}", [P, TPG, 256], f32)) for i in range(2)]
        NU = [ctx.enter_context(nc.psum_tensor(f"NU{i}", [P, 512], f32)) for i in range(2)]
        MID = ctx.enter_context(nc.psum_tensor("MID", [P, 512], f32))
        MTB = ctx.enter_context(nc.psum_tensor("MTB", [P, 512], f32))
        QXf = [q[:].rearrange("p t w -> p (t w)") for q in QX]

        names = """consts_ready edges_zeroed edges_loaded dst_copied pads_stored dst_loaded x_zeroed x_loaded
            weights_in1 weights_in2 lanes_ready lanesT_ready lanesT_used drow_stored pen_stored pen_loaded idx_ready
            wT_ready wT_used wmul_ready prep_done src_ready
            dve act_own pool_own
            idx_copied slot_taken k_used v_kept rows_used
            drow_in0 drow_in1 st_ready expand_done prod_done qwe_kept
            alpha_ready xT_ready scans_ready rows_ready rowscan_ready cols_ready M_ready MT_ready am_ready
            delta_ready fac_psum ident_ready wprep_done we_ready r0_ready tab_kept rescaled gsum_done lin_used p_ready fac_ready msg_ready s_ready nu_ready nu_used factors_ready
            zeroed stats_ready sqrt_done norm_ready h_row hT_psum hT_block tab_psum staged stored0 stored1
            gcn_pre_psum gcn_pre_used
            blk_copied fin_psum fin_used ext_psum ext_used deg_psum deg_sqrt deg_used fin_ready x_ready
            gsum_psum gsum_ready gsq_ready gcn_done h4_row h4_psum h4_block out_stored0 out_stored1 xo_ready
            numT_ready den_ready hT_all deg_ready""".split()
        S = {n: sem(n) for n in names}
        gathered = [sem(f"gathered{g}") for g in range(GPC)]
        qwin_in = [sem(f"qwin_in{g}") for g in range(GPC)]
        NDL = 16 * (3 * HEADS + TPG + 2)
        STORES = [2, 1, 1, 1, 2, 2]
        NWEIGHTS = 6 + 2 * 10 + 4 + 6
        PER = {False: 8, True: 14}
        SBASE = [0, 4 * NG, 5 * NG, NG, 2 * NG, 3 * NG]
        STB = [16 + 16 * NPAIR * sum(STORES[:n + 1]) for n in range(6)]

        block = ctx.enter_context(nc.Block())

        ATT = [dict(k=0, H=1, table=att0_d, width=132, win=q0_d, ww=4, v0=0),
               dict(k=1, H=HEADS, table=kv_d, width=2 * D, win=q_d, ww=132, v0=D),
               dict(k=2, H=HEADS, table=kv_d, width=2 * D, win=q_d, ww=132, v0=D)]
        LIN = [dict(k=0, table=rel_d, idx=relI), dict(k=1, table=gcn_d, idx=srcI), dict(k=2, table=gcn_d, idx=srcI)]
        ORDER = ["att0", "lin0", "lin1", "lin2", "att1", "att2"]
        att_base = lambda a: a["k"] * NG
        stores_before = lambda n: 16 * NPAIR * (n + 1)

        @block.sync
        def _(sp):
            sp.dma_start(dpad[1:E + 1].rearrange("(a b) -> a b", b=E // 125),
                         A["dst"].rearrange("(a b) -> a b", b=E // 125)).then_inc(S["dst_copied"], 16)
            sp.wait_ge(S["x_zeroed"], 1)
            sp.dma_start(xN[:, 0:FULLB, :], A["x"][0:FULLB * P, :].rearrange("(b p) d -> p b d", p=P)
                         ).then_inc(S["x_loaded"], 16)
            sp.dma_start(xN[0:LASTROWS, FULLB, :], A["x"][FULLB * P:N, :]).then_inc(S["x_loaded"], 16)
            full = (NCH - 1) * TPC * P
            rows = (E - full) // P
            sp.wait_ge(S["edges_zeroed"], 1)
            for name, to in (("src", src_in.bitcast(i32)), ("edge_type_8", type_in.bitcast(i32)), ("edge_weight", ew_in)):
                sp.dma_start(to[:, 0:NCH - 1, :], A[name][0:full].rearrange("(c t p) -> t c p", t=TPC, p=P)
                             ).then_inc(S["edges_loaded"], 16)
                sp.dma_start(to[0:rows, NCH - 1, :], A[name][full:full + rows * P].rearrange("(t p) -> t p", p=P)
                             ).then_inc(S["edges_loaded"], 16)
                sp.dma_start(to[rows:rows + 1, NCH - 1, 0:E - full - rows * P],
                             A[name][full + rows * P:E].unsqueeze(0)).then_inc(S["edges_loaded"], 16)
            sp.wait_ge(S["dst_copied"], 16)
            sp.wait_ge(S["pads_stored"], 32)
            for j in range(3):
                v = dpad[j:j + EP].rearrange("(c t p) -> t c p", t=TPC, p=P)
                for h in range(HEADS):
                    sp.dma_start(dst3[j].bitcast(i32)[TPC * h:TPC * h + TPC], v).then_inc(S["dst_loaded"], 16)
            bv = dpad[1:EP + 1].rearrange("(c t p) -> t c p", t=TPC, p=P)
            for r in range(TPG):
                sp.dma_start(base_col.bitcast(i32)[r::TPG, :], bv[::TPG, :, 0]).then_inc(S["dst_loaded"], 16)
            sp.dma_start(baseI[:], dpad[1:EP + 1].rearrange("(g q) -> g q", q=TPG * P)[:, 0].unsqueeze(0)).then_inc(S["dst_loaded"], 16)
            sp.dma_start(nbI[:], dpad[0:EP].rearrange("(c q) -> c q", q=TPC * P)[:, 0].unsqueeze(0)).then_inc(S["dst_loaded"], 16)
            sp.wait_ge(S["lanes_ready"], 1)
            sp.dma_start(drow.rearrange("(c t p) -> t c p", t=TPC, p=P), drow_out).then_inc(S["stored0"], 16)
            sp.wait_ge(S["lanes_ready"], 2)
            sp.dma_start(penrow_d[0].rearrange("c t -> t c"), prefF[0:TPC, :, P - 1]).then_inc(S["stored1"], 16)
            sp.dma_start(penrow_d[1].rearrange("c t -> t c"), prefB[0:TPC, :, 0]).then_inc(S["pen_stored"], 16)
            sp.wait_ge(S["pen_stored"], 16)
            sp.wait_ge(S["stored1"], 16)
            for h in range(HEADS):
                sp.dma_start(penF_row[:, :, h, 1:TPC + 1], penrow_d[0:1]).then_inc(S["pen_loaded"], 16)
                sp.dma_start(penB_in[:, :, h, 0:TPC - 1], penrow_d[1:2, :, 0:TPC - 1]).then_inc(S["pen_loaded"], 16)

            def store_tables(n, parts):
                with sp.Fori(0, NPAIR) as i:
                    for k in range(2):
                        sp.wait_ge(S["staged"], ONE + 2 * NPAIR * n + 2 * i + k + 1)
                        for m, (table, width, off) in enumerate(parts):
                            ins = sp.dma_start(table[ds((2 * i + k) * P, P), :], stage2[k][:, off:off + width])
                            ins.then_inc(S[f"stored{k}"], 16)

            def attention_inputs(a):
                b = att_base(a)
                with sp.Fori(0, NCH) as c:
                    for g in range(GPC):
                        if g % (GPC // 2) == 0:
                            half = g // (GPC // 2)
                            sp.wait_ge(S["st_ready"], ONE + b + GPC * c)
                            sp.dma_start(drow_sb[:, half, :], drow[ds(c * TPC * P + half * TPC * P // 2, TPC * P // 2)]
                                         .unsqueeze(0).broadcast_to([P, TPC * P // 2])).then_inc(S[f"drow_in{half}"], 16)
                        base = sp.value_load(baseI[0:1, ds(c * GPC + g, 1)], min_val=0, max_val=N)
                        sp.wait_ge(S["expand_done"], ONE + b + GPC * c)
                        sp.dma_start(qwin[:, g, 0:a["ww"]], a["win"][ds(base, P), :]).then_inc(qwin_in[g], 16)

            store_tables(0, [(att0_d, 132, 0), (q0_d, 4, 129)])
            sp.wait_ge(S["stored0"], STB[0])
            sp.wait_ge(S["stored1"], STB[0])
            attention_inputs(ATT[0])
            store_tables(1, [(rel_d.rearrange("(n r) d -> n (r d)", r=NREL), NREL * D, 0)])
            store_tables(2, [(gcn_d, D, 0)])
            store_tables(3, [(gcn_d, D, 0)])
            for n, a in ((4, ATT[1]), (5, ATT[2])):
                store_tables(n, [(kv_d, 2 * D, 0), (q_d, 132, 2 * D)])
                sp.wait_ge(S["stored0"], STB[n])
                sp.wait_ge(S["stored1"], STB[n])
                attention_inputs(a)
            sp.wait_ge(S["xo_ready"], ONE + NB)
            sp.dma_start(out[0:FULLB * P, :].rearrange("(b p) d -> p b d", p=P), xN[:, 0:FULLB, :]).then_inc(S["out_stored0"], 16)
            sp.dma_start(out[FULLB * P:N, :], xN[0:LASTROWS, FULLB, :]).then_inc(S["out_stored0"], 16)
            sp.wait_ge(S["out_stored0"], 32)

        @block.gpsimd
        def _(pool):
            own = Tally(S["pool_own"])
            pool.memset(xN[:, FULLB:NB, :], 0.0).then_inc(S["x_zeroed"], 1)
            pool.memset(pads_sb[0:1, 0:1], -1)
            pool.memset(pads_sb[0:1, 1:1 + P], N).then_inc(S["consts_ready"], 1)
            for to in (src_in.bitcast(i32), type_in.bitcast(i32), ew_in):
                last = pool.memset(to[:, NCH - 1, :], 0)
            last.then_inc(S["edges_zeroed"], 1)
            pool.iota(iota_i, [[1, P]], base=0, channel_multiplier=0).then_inc(S["consts_ready"], 1)
            pool.iota(iota_pi[:], [[1, 1]], base=0, channel_multiplier=1).then_inc(S["consts_ready"], 1)
            pool.memset(ones_row[:], 1.0)
            pool.memset(eps_t[:], EPS).then_inc(S["consts_ready"], 1)
            pool.memset(pe8[:], 1.0)
            for q in range(2):
                pool.memset(WeH8[q][:], 0.0)
            pool.memset(penF_row[:], -BIG)
            pool.memset(penB_in, -BIG)
            pool.memset(rin[:], -BIG)
            pool.memset(srcI[:, T:T + TPC], 0)
            pool.memset(relI[:, T:T + TPC], 0)
            pool.memset(alphax[:], 0.0)
            pool.memset(after_row[:], -BIG)
            pool.memset(delta_ext0[:], 0.0)
            pool.memset(extT[:], 0.0).then_inc(S["consts_ready"], 1)

            def gathers(n, table, width, idx, free, base):
                pool.wait_ge(S["stored0"], STB[n])
                pool.wait_ge(S["stored1"], STB[n])
                rows = ring[:, 0:TPC * width].rearrange("p (t w) -> p t w", w=width)
                HG = GPC // 2

                def copy_indices(c, half, done):
                    if half:
                        pool.wait_ge(S[free[-1]], base[-1] + FREE + GPC * c)
                        pool.sem_inc(S["slot_taken"], 1)
                    elif done is not None:
                        for g in range(HG):
                            pool.wait_ge(gathered[g], 16 * TPG * (n * NCH + done))
                            pool.sem_inc(S["slot_taken"], 1)
                    pool.tensor_copy(idx_slot[:, HG * TPG * half:HG * TPG * (half + 1)],
                                     idx[:, ds(c * TPC + HG * TPG * half, HG * TPG)]).then_inc(S["idx_copied"], 1)

                copies = n * (2 * NCH + 1)
                if n:
                    pool.wait_ge(S["idx_copied"], copies)
                copy_indices(0, 0, 0 if n else None)
                with pool.Fori(0, NCH) as c:
                    for g in range(GPC):
                        if g == 3:
                            copy_indices(c, 1, c)
                        if g == 6:
                            copy_indices(c + 1, 0, c + 1)
                        if g % HG == 0:
                            pool.wait_ge(S["idx_copied"], copies + 2 * c + 1 + (g > 0))
                            pool.sem_inc(S["slot_taken"], 1)
                        for s, b in zip(free, base):
                            pool.wait_ge(S[s], b + GPC * c + g + 1)
                            pool.sem_inc(S["slot_taken"], 1)
                        for t in range(TPG * g, TPG * g + TPG):
                            pool.indirect_dma_start(
                                out=rows[:, t, :], out_offset=None, in_=table,
                                in_offset=bass.IndirectOffsetOnAxis(ap=idx_slot[:, t:t + 1].bitcast(u32), axis=0)
                            ).then_inc(gathered[g], 16)

            pool.wait_ge(S["idx_ready"], 2)
            gathers(0, att0_d, 132, srcI, ("v_kept",), (0,))
            gathers(1, rel_d, D, relI, ("rows_used",), (0,))
            gathers(2, gcn_d, D, srcI, ("rows_used",), (NG + FREE,))
            gathers(3, gcn_d, D, srcI, ("rows_used",), (2 * (NG + FREE),))
            gathers(4, kv_d, 2 * D, srcI, ("k_used", "v_kept"), (0, NG + FREE))
            gathers(5, kv_d, 2 * D, srcI, ("k_used", "v_kept"), (NG + FREE, 2 * (NG + FREE)))

        @block.scalar
        def _(act):
            own = Tally(S["act_own"])
            for name in ("st_ready", "staged", "h_row", "qwe_kept"):
                act.sem_inc(S[name], ONE)
            act.wait_ge(S["consts_ready"], 1)
            act.dma_start(dpad[0:1].unsqueeze(0), pads_sb[0:1, 0:1]).then_inc(S["pads_stored"], 16)
            act.dma_start(dpad[E + 1:EP + 2].unsqueeze(0), pads_sb[0:1, 1:EP + 2 - E]).then_inc(S["pads_stored"], 16)

            def load(dst, src):
                act.dma_start(dst, src).then_inc(S["weights_in1"], 16)

            load(W1nat, A["L0_gnn_W1"])
            load(W2nat, A["L0_gnn_W2"])
            load(acol[:, 0:1], A["L0_gnn_a_t"].unsqueeze(1))
            load(acol[:, 1:2], A["L0_gnn_a_s"].unsqueeze(1))
            load(g1nat, A["L2_gnn_W1"])
            load(g2nat, A["L2_gnn_W2"])
            for q in range(2):
                for m, x in enumerate("kvq"):
                    load(Rq[q][:, m * D:(m + 1) * D], A[f"L3_gnn_W{x}{q + 1}"])
                    load(bq[q][:, m * D:(m + 1) * D], A[f"L3_gnn_b{x}{q + 1}"].unsqueeze(0))
                load(Wsk[q][:], A[f"L3_gnn_Ws{q + 1}"])
                load(wecol[:, q:q + 1], A[f"L3_gnn_We{q + 1}"].rearrange("a d -> d a"))
                load(wecol[:, 2 + q:3 + q], A[f"L3_gnn_bq{q + 1}"].unsqueeze(1))
                load(brow[:, 1 + q, :], A[f"L3_gnn_bs{q + 1}"].unsqueeze(0))
            load(basisW, A["L1_gnn_weight"].rearrange("b i o -> i b o"))
            load(wcomp[:], A["L1_gnn_w_comp"].rearrange("r b -> (r b)").unsqueeze(0).broadcast_to([P, NREL * NBASE]))
            load(rootW[:], A["L1_gnn_root_weight"])
            load(brow[:, 0, :], A["L1_gnn_bias"].unsqueeze(0))
            for m, name in enumerate(("b1", "g1", "be1", "b2", "g2", "be2")):
                load(gcol[:, m:m + 1], A[f"L2_gnn_{name}"].unsqueeze(1))

            SC = HD ** -0.5
            act.wait_ge(S["wT_ready"], 1)
            act.copy(R0[:, 0:D], QXf[1][:, 0:D])
            act.copy(R0[:, D:D + 2], QXf[1][:, 3 * D:3 * D + 2]).then_inc(S["r0_ready"], 1)
            act.copy(G1T[:], QXf[1][:, D:2 * D])
            act.copy(G2T[:], QXf[1][:, 2 * D:3 * D])
            act.copy(wqT.rearrange("p a b -> p (a b)"), QXf[1][:, 512:768]).then_inc(S["wT_used"], 1)
            act.wait_ge(S["wmul_ready"], 1)
            for q in range(2):
                act.mul(Rq[q][:, 2 * D:3 * D], Rq[q][:, 2 * D:3 * D], SC)
                act.mul(Rq[q][:, 3 * D:3 * D + 4], QXf[0][:, 512 + 4 * q:516 + 4 * q], SC)
                act.mul(bq[q][:, 2 * D:3 * D], bq[q][:, 2 * D:3 * D], SC)
                act.mul(bq[q][:, 3 * D:3 * D + 4], QXf[0][0:1, 520 + 4 * q:524 + 4 * q], SC)
                act.copy(WeH8T[q][:], QXf[0][0:8, 640 + 128 * q:768 + 128 * q])
            act.copy(facs[:], neg_iota_p[:].broadcast_to([P, 2])).then_inc(S["wprep_done"], 1)

            def deviations(m):
                act.wait_ge(S["stats_ready"], m + 1)
                act.activation(rstd[:], mv[:, :, 1], ACT.Sqrt, bias=eps_t[:]).then_inc(S["sqrt_done"], 1)

            def normed_blocks(i, k, m):
                act.wait_ge(S["hT_psum"], ONE + NB * m + 2 * i)
                act.activation(hrow[:, k, :], xN[:, ds(2 * i + k, 1), :].rearrange("p a d -> p (a d)"), ACT.Relu,
                               bias=nbias[:, ds(2 * i + k, 1)], scale=rstd[:, ds(2 * i + k, 1)]).then_inc(S["h_row"], 1)

            def stage_table(i, k, n):
                act.wait_ge(S["tab_psum"], ONE + NB * n + 2 * i + k + 1)
                act.wait_ge(S[f"stored{k}"], (STB[n - 1] if n else 16) + i * (16 * STORES[n]))
                if n == 0:
                    act.copy(stage2[k][:, 0:132], QXf[k][:, 0:132]).then_inc(S["tab_kept"], 1)
                elif n == 1:
                    act.copy(stage2[k][:, 0:NREL * D], QXf[k][:, 0:NREL * D]).then_inc(S["staged"], 1)
                elif n in (2, 3):
                    act.activation(stage2[k][:, 0:D], QXf[k][:, 0:D], ACT.Copy,
                                   scale=dinvN[:, ds(2 * i + k, 1)]).then_inc(S["staged"], 1)
                else:
                    act.copy(stage2[k][:, 0:388], QXf[k][:, 0:388]).then_inc(S["staged"], 1)

            def norm_tables(m, n):
                deviations(m)
                act.wait_ge(S["norm_ready"], m + 1)
                with act.Fori(0, NPAIR) as i:
                    for k in range(2):
                        normed_blocks(i, k, m)
                    for k in range(2):
                        stage_table(i, k, n)

            def attention(a):
                b, cb, H = att_base(a), a["k"] * NCH, a["H"]
                gb = [0, 4, 5][a["k"]] * 16 * TPG * NCH
                width, v0, L3 = a["width"], a["v0"], a["k"] > 0
                vw = 132 if not L3 else D
                rows = ring[:, 0:TPC * width].rearrange("p (t w) -> p t w", w=width)
                vals = vbuf[:, 0:TPC * vw].rearrange("p (t w) -> p t w", w=vw)
                act.sem_inc(S["v_kept"], FREE)
                with act.Fori(0, NCH) as c:
                    own.enter(c, GPC)
                    for g in range(GPC + 1):
                        if g < GPC:
                            if g % (GPC // 2) == 0:
                                act.wait_ge(S[f"drow_in{g // (GPC // 2)}"], 16 * cb + 16 * (c + 1))
                            q = g % (GPC // 2) * TPG * P
                            act.wait_ge(S["expand_done"], ONE + b + GPC * c + max(g - 1, 0))
                            own.step(act.activation(STa[:, g % 2, :], drow_sb[:, g // (GPC // 2), q:q + TPG * P], ACT.Abs,
                                                    bias=neg_iota_p[:]))
                            act.wait_ge(own.sem, own.value())
                            act.activation(ST[:, g % 2, :], STa[:, g % 2, :], ACT.Relu, bias=1.0, scale=-1.0
                                           ).then_inc(S["st_ready"], 1)
                            act.wait_ge(gathered[g], gb + 16 * TPG * (c + 1))
                            act.wait_ge(S["msg_ready"], ONE + b + GPC * c)
                            act.copy(vals[:, TPG * g:TPG * g + TPG, :], rows[:, TPG * g:TPG * g + TPG, v0:v0 + vw]
                                     ).then_inc(S["v_kept"], 1)
                        if L3 and g:
                            act.wait_ge(S["k_used"], (a["k"] - 1) * (NG + FREE) + FREE + GPC * c + g)
                            act.wait_ge(S["alpha_ready"], ONE + cb + c)
                            act.copy(qwe[:, :, TPG * (g - 1):TPG * g].rearrange("p h t -> p t h"),
                                     QX[(g - 1) % 2][:, :, D:D + HEADS]).then_inc(S["qwe_kept"], 1)
                    own.leave_iteration()
                    act.wait_ge(S["am_ready"], ONE + cb + c + 1)
                    act.wait_ge(S["nu_ready"], ONE + b + GPC * c)
                    rws = H if L3 else 2
                    act.activation(pe8[:, 0:rws, :], am[:, 0:rws, :], ACT.Exp).then_inc(S["p_ready"], 1)
                    act.wait_ge(S["fac_psum"], cb + c + 1)
                    act.wait_ge(S["rescaled"], ONE + cb + c)
                    act.activation(facs[:, 0:1], MTB[:, P:P + 1], ACT.Exp)
                    ex = 8 if L3 else 3
                    act.activation(facs[0:ex, 1:2], MTB[0:ex, P + 1:P + 2], ACT.Exp).then_inc(S["fac_ready"], 1)
                own.leave(NCH)

            def copy_blocks(i, k, f, src):
                b = ds((2 * i + k) * P, P)
                act.wait_ge(S["fin_psum"], ONE + NB * f + 2 * i)
                if f in (1, 3, 4):
                    act.copy(blkT[:, k, :], hT[:, b])
                if f in (3, 4):
                    act.copy(extblk[:, k, :], extT[:, b])
                act.copy(numblk[:, k, :], src[:, b]).then_inc(S["blk_copied"], 1)

            norm_tables(0, 0)
            attention(ATT[0])
            act.wait_ge(S["numT_ready"], 1)
            with act.Fori(0, NPAIR) as i:
                for k in range(2):
                    copy_blocks(i, k, 0, numT)
            act.wait_ge(S["deg_ready"], 1)
            act.activation(dinvN[:], exN[:, :, 2], ACT.Sqrt, bias=1.0).then_inc(S["deg_sqrt"], 1)
            for j in range(13):
                act.wait_ge(S["deg_psum"], j + 1)
                act.activation(dinvT[:, j * 256:(j + 1) * 256], QXf[j % 2][:, 0:256], ACT.Sqrt, bias=1.0
                               ).then_inc(S["deg_sqrt"], 1)
            norm_tables(1, 1)
            act.wait_ge(S["numT_ready"], 2)
            with act.Fori(0, NPAIR) as i:
                for k in range(2):
                    copy_blocks(i, k, 1, numT)
            norm_tables(2, 2)

            def graph_norm(j):
                act.wait_ge(S["numT_ready"], 3 + j)
                act.activation(vbuf[:, 0:N], numT[:, 0:N], ACT.Identity, accum_out=small[:, 0:1]).then_inc(S["gsum_ready"], 1)
                act.wait_ge(S["gsq_ready"], 2 * j + 1)
                act.activation(vbuf[:, 0:N], numT[:, 0:N], ACT.Square, bias=small[:, 2:3], accum_out=small[:, 3:4]
                               ).then_inc(S["gsum_ready"], 1)
                act.wait_ge(S["gsum_psum"], 2 * j + 2)
                act.activation(small[:, 4:5], MTB[:, 1:2], ACT.Sqrt, bias=eps_t[:], scale=1.0 / (N * D)).then_inc(S["sqrt_done"], 1)
                act.wait_ge(S["gsq_ready"], 2 * j + 2)
                act.activation(hT[:], numT[:], ACT.Relu, bias=small[:, 7:8], scale=small[:, 6:7]).then_inc(S["hT_all"], 1)

            graph_norm(0)
            act.wait_ge(S["hT_all"], 1)
            with act.Fori(0, NPAIR) as i:
                for k in range(2):
                    act.wait_ge(S["tab_psum"], ONE + NB * 3 + 2 * i)
                    act.copy(blkT[:, k, :], hT[:, ds((2 * i + k) * P, P)]).then_inc(S["hT_block"], 1)
                for k in range(2):
                    stage_table(i, k, 3)
            graph_norm(1)
            act.wait_ge(S["hT_all"], 2)
            with act.Fori(0, NPAIR) as i:
                for k in range(2):
                    copy_blocks(i, k, 2, hT)
            norm_tables(3, 4)
            attention(ATT[1])
            act.wait_ge(S["numT_ready"], 5)
            with act.Fori(0, NPAIR) as i:
                for k in range(2):
                    copy_blocks(i, k, 3, numT)
                for k in range(2):
                    stage_table(i, k, 5)
            attention(ATT[2])
            act.wait_ge(S["numT_ready"], 6)
            with act.Fori(0, NPAIR) as i:
                for k in range(2):
                    copy_blocks(i, k, 4, numT)

        @block.vector
        def _(dve):
            d = Tally(S["dve"])
            for name in ("msg_ready", "alpha_ready", "nu_used", "hT_block", "fin_used", "rescaled", "am_ready", "xo_ready", "lin_used"):
                dve.sem_inc(S[name], ONE)

            def then(ins):
                dve.wait_ge(d.sem, d.step(ins))

            def tt(o, x, y, op):
                return dve.tensor_tensor(o, x, y, op)

            dve.wait_ge(S["consts_ready"], 5)
            dve.tensor_copy(iota_j[:], iota_i)
            then(dve.tensor_copy(small[:, 15:16], iota_pi[:]))
            dve.tensor_scalar(neg_iota_p[:], small[:, 15:16], -1.0, None, ALU.mult)
            dve.tensor_scalar(ident[:], iota_j[:], small[:, 15:16], None, ALU.is_equal).then_inc(S["ident_ready"], 1)
            dve.memset(ones_f[:], 1.0)
            then(dve.memset(headmask[:], 0.0))
            for h in range(HEADS):
                last = dve.memset(headmask[HD * h:HD * (h + 1), h:h + 1], 1.0)
            then(last)
            then(dve.tensor_copy(sel_deg[:], ident[0:8, 2:3].broadcast_to([8, P])))
            dve.wait_ge(S["edges_loaded"], 16 * 9)
            dve.tensor_copy(src_in, src_in.bitcast(i32)).then_inc(S["src_ready"], 1)
            dve.tensor_copy(type_in, type_in.bitcast(i32)).then_inc(S["src_ready"], 1)
            dve.wait_ge(S["weights_in1"], 16 * NWEIGHTS)
            for q in range(2):
                dve.tensor_scalar(WeH8[q][:, 4:8], headmask[:], wecol[:, q:q + 1], None, ALU.mult).then_inc(S["we_ready"], 1)
            dve.wait_ge(S["dst_loaded"], NDL)
            i3 = [x.bitcast(i32) for x in dst3]
            then(tt(dst_rel, i3[1][0:TPC], base_col.bitcast(i32).unsqueeze(2).broadcast_to([TPC, NCH, P]), ALU.subtract))
            dve.tensor_copy(drow_out, dst_rel)
            tt(dst3[0], i3[1], i3[0], ALU.not_equal)
            then(tt(dst3[2], i3[1], i3[2], ALU.not_equal))
            dve.tensor_scalar(nbI[:], nbI[:], 0, None, ALU.max)
            dve.tensor_scalar(cont_row[:], dst3[0][0:1, :, 0], -1.0, 1.0, ALU.mult, ALU.add).then_inc(S["lanes_ready"], 1)
            dve.tensor_scalar(fpen[:], dst3[0], -BIG, None, ALU.mult)
            then(dve.tensor_scalar(bpen[:, :, ::-1], dst3[2], -BIG, None, ALU.mult))
            for c in range(NCH):
                dve.tensor_tensor_scan(prefF[:, c, :], ones_f[:], fpen[:, c, :], 0.0, ALU.mult, ALU.add)
                last = dve.tensor_tensor_scan(prefB[:, c, ::-1], ones_f[:], bpen[:, c, :], 0.0, ALU.mult, ALU.add)
            last.then_inc(S["lanes_ready"], 1)
            dve.wait_ge(S["lanesT_ready"], 5)
            then(dve.tensor_copy(srcI[:, 0:T], MID[:, 0:T]))
            dve.scalar_tensor_tensor(relI[:, 0:T], srcI[:, 0:T], float(NREL), MTB[:, 0:T], ALU.mult, ALU.add)
            dve.tensor_copy(ewP[:], QXf[0][:, 0:T])
            dve.tensor_copy(dstP[:], NU[0][:, 0:T])
            dve.tensor_copy(startP[:], NU[1][:, 0:T]).then_inc(S["idx_ready"], 2)
            dve.memset(numT[:], 0.0).then_inc(S["zeroed"], 1)
            dve.wait_ge(S["pen_loaded"], 16 * 2 * HEADS)
            then(dve.tensor_copy(penB_row[:].rearrange("q c h t -> q (c h) t")[:, :, ::-1],
                                 penB_in.rearrange("q c h t -> q (c h) t")))
            dve.wait_ge(S["r0_ready"], 1)
            then(tt(R0[:, 130:131], R0[:, 128:129], R0[:, 129:130], ALU.add))
            dve.tensor_scalar(R0[:, 131:132], R0[:, 130:131], 0.2, None, ALU.mult).then_inc(S["r0_ready"], 1)

            def norm_stats(m):
                for b in range(NB):
                    last = dve.bn_stats(stats[:, b, :], xN[:, b, :])
                then(last)
                for b in range(NB):
                    last = dve.bn_aggr(mv[:, b, :], stats[:, b, :])
                last.then_inc(S["stats_ready"], 1)
                dve.wait_ge(S["sqrt_done"], m + 1 + (2 if m == 3 else 0))
                then(dve.reciprocal(rstd[:], rstd[:]))
                dve.scalar_tensor_tensor(nbias[:], mv[:, :, 0], -1.0, rstd[:], ALU.mult, ALU.mult).then_inc(S["norm_ready"], 1)

            def transposed_block(i, k, m, n, to):
                dve.wait_ge(S["hT_psum"], ONE + NB * m + 2 * i + k + 1)
                if n:
                    dve.tensor_copy(hT[:, ds((2 * i + k) * P, P)], NU[k][:, 256:384])
                dve.wait_ge(S["tab_psum"], ONE + NB * n + 2 * i)
                dve.tensor_copy(to[:, k, :], NU[k][:, 256:384]).then_inc(S["hT_block"], 1)

            def norm_tables(m, n):
                norm_stats(m)
                with dve.Fori(0, NPAIR) as i:
                    for k in range(2):
                        transposed_block(i, k, m, n, blkT)
                    if n == 0:
                        for k in range(2):
                            dve.wait_ge(S["tab_kept"], 2 * i + k + 1)
                            dve.tensor_copy(wx[:, ds(2 * i + k, 1), :].rearrange("p a d -> p (a d)"), QXf[k][:, 0:D])
                            tt(stage2[k][:, 132:133], stage2[k][:, 130:131], stage2[k][:, 131:132], ALU.max
                               ).then_inc(S["staged"], 1)

            def attention(a):
                b, cb, H = att_base(a), a["k"] * NCH, a["H"]
                L3 = a["k"] > 0
                LN = P
                gb = [0, 4, 5][a["k"]] * 16 * TPG * NCH
                kb = (a["k"] - 1) * (NG + FREE) + FREE
                vb = a["k"] * (NG + FREE) + FREE
                vw = 132 if not L3 else D
                ex = 8 if L3 else 3
                vals = vbuf[:, 0:TPC * vw].rearrange("p (t w) -> p t w", w=vw)
                rows = ring4
                for k in range(2):
                    dve.wait_ge(S[f"stored{k}"], STB[(0, 4, 5)[a["k"]]])
                if L3:
                    dve.sem_inc(S["k_used"], FREE)
                then(dve.memset(rin[:], -BIG))
                with dve.Fori(0, NCH) as c:
                    d.enter(c, PER[a["k"] > 0])
                    base = [dve.value_load(baseI[0:1, ds(c * GPC + g, 1)], min_val=0, max_val=N) for g in range(GPC)]
                    shared = dve.value_load(nbI[0:1, ds(c, 1)], min_val=0, max_val=N)

                    def onehots(g0, g1):
                        for g in range(g0, g1):
                            tt(Sb[:, g], iota_j[:].unsqueeze(1).broadcast_to([P, TPG, P]),
                               dstP[:, ds(c * TPC + TPG * g, TPG)].unsqueeze(2).broadcast_to([P, TPG, P]),
                               ALU.is_equal).then_inc(S["s_ready"], 1)

                    if L3:
                        def head_sums(g):
                            dve.wait_ge(S["k_used"], kb + GPC * c + g + 1)
                            d.step(dve.tensor_reduce(
                                alphax[:, :, TPG * g:TPG * g + TPG].rearrange("p h t -> p t h"),
                                prod[:, g % 2, :].rearrange("p (t h d) -> p t h d", t=TPG, h=HEADS), AX.X, ALU.add))

                        for g in range(GPC):
                            dve.wait_ge(S["expand_done"], ONE + b + GPC * c + g + 1)
                            dve.wait_ge(gathered[g], gb + 16 * TPG * (c + 1))
                            if g >= 2:
                                dve.wait_ge(d.sem, d.value())
                            tt(prod[:, g % 2, :].rearrange("p (t w) -> p t w", w=D), QX[g % 2][:, :, 0:D],
                               rows[:, TPG * g:TPG * g + TPG, 0:D], ALU.mult).then_inc(S["k_used"], 1)
                            if g:
                                head_sums(g - 1)
                        head_sums(GPC - 1)
                        dve.wait_ge(S["qwe_kept"], ONE + (a["k"] - 1) * NG + GPC * c + GPC)
                        then(tt(am[:], qwe[:], ewP[:, ds(c * TPC, TPC)].unsqueeze(1).broadcast_to([P, HEADS, TPC]), ALU.mult))
                        tt(alpha[:], am[:], alphax[:], ALU.add).then_inc(S["alpha_ready"], 1)
                        dve.wait_ge(S["alpha_ready"], ONE + cb + c + 1)
                        scan_in = alpha
                    else:
                        dve.wait_ge(S["expand_done"], ONE + b + GPC * c + GPC)
                        dve.wait_ge(S["v_kept"], vb + GPC * c + GPC)
                        qx = QXf[0][:, 0:4 * TPC].rearrange("p (t w) -> p t w", w=4)
                        then(tt(qwe[:, 0, :], vals[:, :, D], qx[:, :, 0], ALU.add))
                        then(dve.scalar_tensor_tensor(alpha[:, 0, :], qwe[:, 0, :], 0.2, qwe[:, 0, :], ALU.mult, ALU.max))
                        tt(alphax[:, 0, :], alpha[:, 0, :], qx[:, :, 3], ALU.max).then_inc(S["alpha_ready"], 1)
                    onehots(0, 2)
                    dve.wait_ge(S["xT_ready"], cb + c + 1)
                    fp = fpen[0:LN, ds(c, 1), :].rearrange("p a d -> p (a d)")
                    bp = bpen[0:LN, ds(c, 1), :].rearrange("p a d -> p (a d)")
                    dve.tensor_tensor_scan(Fs[0:LN, :], fp, MID[0:LN, 0:P], -BIG, ALU.add, ALU.max)
                    dve.tensor_tensor_scan(Bs[0:LN, ::-1], bp, MID[0:LN, P - 1::-1], -BIG, ALU.add, ALU.max
                                           ).then_inc(S["scans_ready"], 1)
                    onehots(2, 4)
                    dve.wait_ge(S["rows_ready"], cb + c + 1)
                    then(dve.tensor_copy(rin[:, :, 1:TPC + 1], MID[0:1, P:P + LN].rearrange("p (h t) -> p h t", h=HEADS)))
                    penF = penF_row[:, ds(c, 1), :, :].rearrange("p a h t -> p (a h t)")
                    penB = penB_row[:, ds(c, 1), :, :].rearrange("p a h t -> p (a h t)")
                    flat = lambda x: x[:, :, :].rearrange("p h t -> p (h t)")
                    then(dve.tensor_tensor_scan(flat(SF), penF, flat(rin), -BIG, ALU.add, ALU.max))
                    byh = lambda x: x[:, 0:LN].rearrange("p (h t) -> p h t", h=HEADS)
                    dve.tensor_copy(byh(before_row), SF[:, :, 0:TPC])
                    sbk = sbrow[:, 0:LN]
                    then(dve.tensor_tensor_scan(sbk[:, ::-1], penB, MID[0:1, 2 * P + LN - 1:2 * P - 1:-1], -BIG,
                                                ALU.add, ALU.max))
                    dve.tensor_copy(byh(after_row)[:, :, 0:TPC - 1], byh(sbrow)[:, :, 1:TPC]).then_inc(S["rowscan_ready"], 1)
                    onehots(4, 6)
                    dve.wait_ge(S["cols_ready"], cb + c + 1)
                    pf = prefF[0:LN, ds(c, 1), :].rearrange("p a d -> p (a d)")
                    pb = prefB[0:LN, ds(c, 1), :].rearrange("p a d -> p (a d)")
                    dve.scalar_tensor_tensor(Ms[0:LN, :], pf, MID[0:LN, 384:385], Fs[0:LN, :], ALU.add, ALU.max)
                    then(dve.scalar_tensor_tensor(M2s[0:LN, :], pb, MID[0:LN, 385:386], Bs[0:LN, :], ALU.add, ALU.max))
                    tt(Ms[0:LN, :], Ms[0:LN, :], M2s[0:LN, :], ALU.max).then_inc(S["M_ready"], 1)
                    onehots(6, 8)
                    dve.wait_ge(S["MT_ready"], cb + c + 1)
                    mt = MTB[:, 0:LN].rearrange("p (h t) -> p h t", h=HEADS)
                    last = tt(am[:, 0:H, :], alpha[:, 0:H, :], mt[:, 0:H, :], ALU.subtract)
                    if not L3:
                        then(dve.tensor_copy(am[:, 2, :], mt[:, 0, :]))
                        last = tt(am[:, 1, :], qx[:, :, 3], am[:, 2, :], ALU.subtract)
                    last.then_inc(S["am_ready"], 1)
                    dl = delta[:, :, 0:H]
                    mnew = MTB[0:1, 0:LN].rearrange("p (h t) -> p h t", h=HEADS)[:, 0:H, 0].unsqueeze(1).broadcast_to([1, 2, H])
                    then(tt(dl, rin[:, 0:H, 0].unsqueeze(1).broadcast_to([1, 2, H]), mnew, ALU.subtract))
                    dve.tensor_scalar(delta_feat[:].rearrange("p (h d) -> p h d", h=H),
                                      dl[:, 0, :].unsqueeze(2).broadcast_to([1, H, D // H]),
                                      cont_row[:, ds(c, 1)], None, ALU.mult)
                    dve.tensor_scalar((delta_ext3 if L3 else delta_ext0)[:, 0:2 * H].rearrange("p (a h) -> p a h", h=H), dl,
                                      cont_row[:, ds(c, 1)], None, ALU.mult).then_inc(S["delta_ready"], 1)
                    dve.tensor_copy(rin[:, 0:HEADS, 0:1], SF[:, 0:HEADS, TPC:TPC + 1])
                    dve.wait_ge(S["fac_ready"], cb + c + 1)
                    dve.wait_ge(S["nu_used"], ONE + b + GPC * c)
                    dve.tensor_scalar(numT[:, ds(shared, 1)], numT[:, ds(shared, 1)], facs[:, 0:1], None, ALU.mult)
                    dve.tensor_scalar(extT[0:ex, ds(shared, 1)], extT[0:ex, ds(shared, 1)], facs[0:ex, 1:2], None, ALU.mult
                                      ).then_inc(S["rescaled"], 1)
                    dve.wait_ge(S["p_ready"], cb + c + 1)
                    if L3:
                        tt(pe8[:, HEADS:2 * HEADS, :], pe8[:, 0:HEADS, :],
                           ewP[:, ds(c * TPC, TPC)].unsqueeze(1).broadcast_to([P, HEADS, TPC]), ALU.mult).then_inc(S["factors_ready"], 1)
                    else:
                        tt(pe8[:, 1, :], pe8[:, 1, :], startP[:, ds(c * TPC, TPC)], ALU.mult).then_inc(S["factors_ready"], 1)
                    dve.wait_ge(S["rescaled"], ONE + cb + c + 1)

                    def add_sums(g):
                        dve.wait_ge(S["nu_ready"], ONE + b + GPC * c + g + 1)
                        dve.wait_ge(S["nu_used"], ONE + b + GPC * c + g)
                        w = ds(base[g], P)
                        tt(numT[:, w], numT[:, w], NU[g % 2][:, 0:P], ALU.add)
                        tt(extT[0:ex, w], extT[0:ex, w], NU[g % 2][0:ex, P:2 * P], ALU.add).then_inc(S["nu_used"], 1)

                    for g in range(GPC):
                        dve.wait_ge(S["v_kept"], vb + GPC * c + g + 1)
                        dve.wait_ge(S["nu_ready"], ONE + b + GPC * c + max(g - 1, 0))
                        v = vals[:, TPG * g:TPG * g + TPG, 0:D].rearrange("p t (h d) -> p t h d", h=H)
                        f = pe8[:, 0:H, TPG * g:TPG * g + TPG].rearrange("p h t -> p t h").unsqueeze(3).broadcast_to([P, TPG, H, D // H])
                        tt(msg[:, g % 2].rearrange("p t (h d) -> p t h d", h=H), v, f, ALU.mult).then_inc(S["msg_ready"], 1)
                        if g:
                            add_sums(g - 1)
                    add_sums(GPC - 1)
                    d.leave_iteration()
                d.leave(NCH)
                dve.wait_ge(S["nu_used"], ONE + b + NG)

            def linear(p):
                b = p["k"] * NG
                for k in range(2):
                    dve.wait_ge(S[f"stored{k}"], STB[1 + p["k"]])
                with dve.Fori(0, NCH) as c:
                    base = [dve.value_load(baseI[0:1, ds(c * GPC + g, 1)], min_val=0, max_val=N) for g in range(GPC)]
                    for g in range(GPC):
                        if g == 0:
                            dve.wait_ge(S["rows_used"], p["k"] * (NG + FREE) + FREE + GPC * c)
                        tt(Sb[:, g], iota_j[:].unsqueeze(1).broadcast_to([P, TPG, P]),
                           dstP[:, ds(c * TPC + TPG * g, TPG)].unsqueeze(2).broadcast_to([P, TPG, P]),
                           ALU.is_equal).then_inc(S["s_ready"], 1)
                    for g in range(GPC):
                        dve.wait_ge(S["rows_used"], p["k"] * (NG + FREE) + FREE + GPC * c + g + 1)
                        dve.wait_ge(S["lin_used"], ONE + b + GPC * c + g)
                        w = ds(base[g], P)
                        tt(numT[:, w], numT[:, w], NU[g % 2][:, 0:P], ALU.add).then_inc(S["lin_used"], 1)
                dve.wait_ge(S["lin_used"], ONE + b + NG)

            def extras():
                dve.wait_ge(S["ext_psum"], EXT[0] + 1)
                EXT[0] += 1
                then(dve.tensor_copy(exN[:].rearrange("p b e -> p (b e)"), MID[:, 0:8 * NB]))

            EXT = [0]
            dve.wait_ge(S["x_loaded"], 32)
            norm_tables(0, 0)
            attention(ATT[0])
            dve.memset(done_mark[:], 0.0).then_inc(S["numT_ready"], 1)
            extras()
            dve.memset(done_mark[:], 0.0).then_inc(S["deg_ready"], 1)
            then(dve.tensor_scalar(exN2[:, :, 0], exN[:, :, 0], 0.0, None, ALU.is_equal))
            then(tt(exN2[:, :, 1], exN[:, :, 1], exN2[:, :, 0], ALU.add))
            then(tt(exN2[:, :, 2], exN[:, :, 0], exN2[:, :, 1], ALU.add))
            then(dve.reciprocal(exN2[:, :, 3], exN2[:, :, 2]))
            with dve.Fori(0, NPAIR) as i:
                d.enter(i, 2)
                for k in range(2):
                    b = ds(2 * i + k, 1)
                    dve.wait_ge(S["fin_psum"], ONE + 2 * i + k + 1)
                    dve.scalar_tensor_tensor(tmpA[:, k, :], wx[:, b, :].rearrange("p a d -> p (a d)"), exN2[:, b, 1], NU[k][:, 0:P],
                                             ALU.mult, ALU.add).then_inc(S["fin_used"], 1)
                    dve.wait_ge(S["fin_used"], ONE + 2 * i + k + 1)
                    xb = xN[:, b, :].rearrange("p a d -> p (a d)")
                    d.step(dve.scalar_tensor_tensor(xb, tmpA[:, k, :], exN2[:, b, 3], xb, ALU.mult, ALU.add))
                d.leave_iteration()
            d.leave(NPAIR)
            dve.wait_ge(d.sem, d.value())
            dve.wait_ge(S["deg_sqrt"], 14)
            dve.reciprocal(dinvN[:], dinvN[:])
            then(dve.reciprocal(dinvT[:], dinvT[:]))
            dve.memset(numT[:], 0.0)
            for q in range(NBASE):
                for r in range(NREL):
                    co = wcomp[:, NBASE * r + q:NBASE * r + q + 1]
                    if q == 0:
                        last = dve.tensor_scalar(Wr[:, r, :], basisW[:, 0, :], co, None, ALU.mult)
                    else:
                        last = dve.scalar_tensor_tensor(Wr[:, r, :], basisW[:, q, :], co, Wr[:, r, :], ALU.mult, ALU.add)
                then(last)
            dve.memset(done_mark[:], 0.0).then_inc(S["zeroed"], 1)
            norm_tables(1, 1)
            linear(LIN[0])
            dve.memset(done_mark[:], 0.0).then_inc(S["numT_ready"], 1)
            with dve.Fori(0, NPAIR) as i:
                for k in range(2):
                    xb = xN[:, ds(2 * i + k, 1), :].rearrange("p a d -> p (a d)")
                    dve.wait_ge(S["fin_psum"], ONE + NB + 2 * i + k + 1)
                    dve.scalar_tensor_tensor(xb, NU[k][:, 0:P], 0.0, xb, ALU.max, ALU.add).then_inc(S["fin_used"], 1)
            dve.wait_ge(S["fin_used"], ONE + 2 * NB)
            then(dve.memset(numT[:], 0.0))
            norm_tables(2, 2)

            def graph_layer(j):
                for q in range(13):
                    dve.wait_ge(S["gcn_pre_psum"], 13 * j + q + 1)
                    w = slice(256 * q, 256 * q + 256)
                    tt(hdT[:, w], QXf[q % 2][:, 0:256], dinvT[:, w], ALU.mult).then_inc(S["gcn_pre_used"], 1)
                linear(LIN[1 + j])
                then(tt(numT[:], numT[:], hdT, ALU.add))
                tt(numT[:], numT[:], dinvT, ALU.mult).then_inc(S["numT_ready"], 1)
                dve.wait_ge(S["gsum_ready"], 2 * j + 1)
                bc, gc, bec = (gcol[:, 3 * j + m:3 * j + m + 1] for m in range(3))
                dve.scalar_tensor_tensor(small[:, 1:2], bc, float(N), small[:, 0:1], ALU.mult, ALU.add
                                         ).then_inc(S["gsum_done"], 1)
                dve.wait_ge(S["gsum_psum"], 2 * j + 1)
                dve.scalar_tensor_tensor(small[:, 2:3], MTB[:, 0:1], -1.0 / (N * D), bc, ALU.mult, ALU.add).then_inc(S["gsq_ready"], 1)
                dve.wait_ge(S["sqrt_done"], 3 + j + 1)
                then(dve.reciprocal(small[:, 5:6], small[:, 4:5]))
                then(tt(small[:, 6:7], small[:, 5:6], gc, ALU.mult))
                dve.scalar_tensor_tensor(small[:, 7:8], small[:, 2:3], small[:, 6:7], bec, ALU.mult, ALU.add
                                         ).then_inc(S["gsq_ready"], 1)
                dve.wait_ge(S["hT_all"], j + 1)
                then(dve.memset(numT[:], 0.0))

            graph_layer(0)
            graph_layer(1)
            with dve.Fori(0, NPAIR) as i:
                for k in range(2):
                    xb = xN[:, ds(2 * i + k, 1), :].rearrange("p a d -> p (a d)")
                    dve.wait_ge(S["fin_psum"], ONE + 2 * NB + 2 * i + k + 1)
                    tt(xb, NU[k][:, 0:P], xb, ALU.add).then_inc(S["fin_used"], 1)
            dve.wait_ge(S["fin_used"], ONE + 3 * NB)
            then(dve.memset(extT[:], 0.0))
            norm_tables(3, 4)
            for j in range(2):
                attention(ATT[1 + j])
                dve.memset(done_mark[:], 0.0).then_inc(S["numT_ready"], 1)
                extras()
                then(dve.tensor_scalar(exN2[:, :, 0:4], exN[:, :, 0:4], 1e-30, None, ALU.max))
                then(dve.reciprocal(exN2[:, :, 4:8], exN2[:, :, 0:4]))
                with dve.Fori(0, NPAIR) as i:
                    d.enter(i, 2 + 2 * j)
                    for k in range(2):
                        b = ds(2 * i + k, 1)
                        dve.wait_ge(S["fin_psum"], ONE + (3 + j) * NB + 2 * i + k + 1)
                        rden = exN2[:, b, 4:8].rearrange("p a h -> p (a h)").unsqueeze(2).broadcast_to([P, HEADS, HD])
                        then(tt(tmpA[:, k, :].rearrange("p (h d) -> p h d", h=HEADS),
                                NU[k][:, 0:P].rearrange("p (h d) -> p h d", h=HEADS), rden, ALU.mult))
                        if j == 0:
                            dve.wait_ge(S["hT_psum"], ONE + 4 * NB + 2 * i)
                            tt(hrow[:, k, :], tmpA[:, k, :], NU[k][:, P:2 * P], ALU.add).then_inc(S["h_row"], 1)
                        else:
                            then(tt(tmpA[:, k, :], tmpA[:, k, :], NU[k][:, P:2 * P], ALU.add))
                            xb = xN[:, b, :].rearrange("p a d -> p (a d)")
                            tt(xb, tmpA[:, k, :], xb, ALU.add).then_inc(S["xo_ready"], 1)
                    d.leave_iteration()
                    for k in range(2 if j == 0 else 0):
                        transposed_block(i, k, 4, 5, blk2)
                d.leave(NPAIR)
                if j == 0:
                    dve.wait_ge(S["fin_psum"], ONE + 4 * NB)
                    dve.memset(numT[:], 0.0)
                    then(dve.memset(extT[:], 0.0))

        @block.tensor
        def _(pe):
            I = ident
            for name in ("expand_done", "nu_ready", "hT_psum", "tab_psum", "fin_psum"):
                pe.sem_inc(S[name], ONE)

            def mm(o, l, r, start=True, stop=True):
                return pe.matmul(o, l, r, start=start, stop=stop)

            pe.wait_ge(S["ident_ready"], 1)
            pe.wait_ge(S["src_ready"], 2)
            for x, to in ((src_in, MID[:]), (type_in, MTB[:]), (ew_in, QXf[0])):
                for c in range(NCH):
                    last = pe.transpose(to[:, TPC * c:TPC * (c + 1)], x[:, c, :], I[0:TPC, 0:TPC])
                last.then_inc(S["lanesT_ready"], 1)
            pe.wait_ge(S["weights_in1"], 16 * NWEIGHTS)
            pe.transpose(QXf[1][:, 0:D], W1nat, I[:])
            pe.transpose(QXf[1][:, D:2 * D], g1nat, I[:])
            pe.transpose(QXf[1][:, 2 * D:3 * D], g2nat, I[:])
            mm(QXf[1][:, 3 * D:3 * D + 1], W1nat, acol[:, 0:1])
            mm(QXf[1][:, 3 * D + 1:3 * D + 2], W2nat, acol[:, 1:2])
            for q in range(2):
                last = pe.transpose(QXf[1][:, 512 + D * q:512 + D * (q + 1)], Rq[q][:, 2 * D:3 * D], I[:])
            last.then_inc(S["wT_ready"], 1)
            pe.wait_ge(S["lanes_ready"], 1)
            for x, to in ((dst_rel, NU[0][:]), (dst3[0][0:TPC], NU[1][:])):
                for c in range(NCH):
                    last = pe.transpose(to[:, TPC * c:TPC * (c + 1)], x[:, c, :], I[0:TPC, 0:TPC])
                last.then_inc(S["lanesT_ready"], 1)
            pe.wait_ge(S["wT_used"], 1)
            pe.wait_ge(S["we_ready"], 2)
            for q in range(2):
                mm(QXf[0][:, 512 + 4 * q:516 + 4 * q], wqT[:, q, :], WeH8[q][:, 4:8])
                mm(QXf[0][0:1, 520 + 4 * q:524 + 4 * q], wecol[:, 2 + q:3 + q], WeH8[q][:, 4:8])
                last = pe.transpose(QXf[0][0:8, 640 + 128 * q:768 + 128 * q], WeH8[q][:], I[:])
            last.then_inc(S["wmul_ready"], 1)
            pe.wait_ge(S["wprep_done"], 1)
            pe.wait_ge(S["idx_ready"], 2)
            pe.wait_ge(S["r0_ready"], 2)

            def transpose_row(i, k, m, n):
                pe.wait_ge(S["h_row"], ONE + NB * m + 2 * i + k + 1)
                pe.wait_ge(S["hT_block"], ONE + NB * n + 2 * i)
                pe.transpose(NU[k][:, 256:384], hrow[:, k, :], I[:]).then_inc(S["hT_psum"], 1)

            def table_block(i, k, n, block):
                pe.wait_ge(S["hT_block"], ONE + NB * n + 2 * i + k + 1)
                pe.wait_ge(S["staged"], ONE + NB * n + 2 * i)
                h = block[:, k, :]
                if n == 0:
                    last = mm(QXf[k][:, 0:132], h, R0[:])
                elif n == 1:
                    w = Wr[:].rearrange("p r d -> p (r d)")
                    mm(QXf[k][:, 0:512], h, w[:, 0:512])
                    last = mm(QXf[k][:, 512:1024], h, w[:, 512:1024])
                elif n in (2, 3):
                    last = mm(QXf[k][:, 0:D], h, (G1T, G2T)[n - 2][:])
                else:
                    mm(QXf[k][:, 0:388], h, Rq[n - 4][:], stop=False)
                    last = mm(QXf[k][:, 0:388], ones_row[:], bq[n - 4][:], start=False)
                last.then_inc(S["tab_psum"], 1)

            def norm_tables(m, n):
                with pe.Fori(0, NPAIR) as i:
                    for k in range(2):
                        transpose_row(i, k, m, n)
                    for k in range(2):
                        table_block(i, k, n, blkT)

            def attention(a):
                b, cb, H = att_base(a), a["k"] * NCH, a["H"]
                L3 = a["k"] > 0
                LN = P
                ex = 8 if L3 else 3
                kb = (a["k"] - 1) * (NG + FREE) + FREE
                sb0 = SBASE[a["k"]]
                with pe.Fori(0, NCH) as c:
                    for g in range(GPC):
                        pe.wait_ge(S["st_ready"], ONE + b + GPC * c + g + 1)
                        pe.wait_ge(qwin_in[g], 16 * cb + 16 * (c + 1))
                        if L3:
                            pe.wait_ge(S["k_used"], kb + GPC * c + max(g - 1, 0))
                            pe.wait_ge(S["qwe_kept"], ONE + (a["k"] - 1) * NG + GPC * c + max(g - 1, 0))
                        elif g == 0:
                            pe.wait_ge(S["am_ready"], ONE + cb + c)
                        for t in range(TPG):
                            to = QX[g % 2][:, t, 0:132] if L3 else QXf[0][:, 4 * (TPG * g + t):4 * (TPG * g + t) + 4]
                            last = mm(to, ST[:, g % 2, t * P:(t + 1) * P], qwin[:, g, 0:a["ww"]])
                        last.then_inc(S["expand_done"], 1)
                    pe.wait_ge(S["alpha_ready"], ONE + cb + c + 1)
                    x = (alpha if L3 else alphax)[:].rearrange("p h t -> p (h t)")
                    pe.transpose(MID[0:LN, 0:P], x, I[:]).then_inc(S["xT_ready"], 1)
                    pe.wait_ge(S["scans_ready"], cb + c + 1)
                    mm(MID[0:1, P:P + LN], Fs[0:LN, P - 1:P], I[0:LN, 0:LN])
                    mm(MID[0:1, 2 * P:2 * P + LN], Bs[0:LN, 0:1], I[0:LN, 0:LN]).then_inc(S["rows_ready"], 1)
                    pe.wait_ge(S["rowscan_ready"], cb + c + 1)
                    mm(MID[0:LN, 384:385], before_row[:, 0:LN], ones_row[:, 0:1])
                    mm(MID[0:LN, 385:386], after_row[:, 0:LN], ones_row[:, 0:1]).then_inc(S["cols_ready"], 1)
                    pe.wait_ge(S["M_ready"], cb + c + 1)
                    pe.transpose(MTB[:, 0:LN], Ms[0:LN, :], I[0:LN, 0:LN]).then_inc(S["MT_ready"], 1)
                    pe.wait_ge(S["delta_ready"], cb + c + 1)
                    mm(MTB[:, P:P + 1], delta_feat[:], ones_row[:, 0:1])
                    mm(MTB[0:ex, P + 1:P + 2], (delta_ext3 if L3 else delta_ext0)[:, 0:ex], ones_row[:, 0:1]
                       ).then_inc(S["fac_psum"], 1)
                    pe.wait_ge(S["factors_ready"], cb + c + 1)
                    for g in range(GPC):
                        pe.wait_ge(S["s_ready"], sb0 + GPC * c + g + 1)
                        pe.wait_ge(S["nu_used"], ONE + b + GPC * c + max(g - 1, 0))
                        for t in range(TPG):
                            last = mm(NU[g % 2][0:ex, P:2 * P], pe8[:, 0:ex, TPG * g + t], Sb[:, g, t, :], t == 0, t == TPG - 1)
                        pe.wait_ge(S["msg_ready"], ONE + b + GPC * c + g + 1)
                        for t in range(TPG):
                            last = mm(NU[g % 2][:, 0:P], msg[:, g % 2, t, :], Sb[:, g, t, :], t == 0, t == TPG - 1)
                        last.then_inc(S["nu_ready"], 1)

            def linear(p, n):
                b, sb0 = p["k"] * NG, SBASE[3 + p["k"]]
                rows = ring[:, 0:TPC * D].rearrange("p (t w) -> p t w", w=D)
                pe.sem_inc(S["rows_used"], FREE)
                with pe.Fori(0, NCH) as c:
                    for g in range(GPC):
                        pe.wait_ge(gathered[g], n * 16 * TPG * NCH + 16 * TPG * (c + 1))
                        pe.wait_ge(S["s_ready"], sb0 + GPC * c + g + 1)
                        pe.wait_ge(S["lin_used"], ONE + b + GPC * c + max(g - 1, 0))
                        for t in range(TPG):
                            last = mm(NU[g % 2][:, 0:P], rows[:, TPG * g + t, :], Sb[:, g, t, :], t == 0, t == TPG - 1)
                        last.then_inc(S["rows_used"], 1)

            def transposes_of_extras(j):
                pe.wait_ge(S["numT_ready"], (1, 5, 6)[j])
                for b in range(NB):
                    last = pe.transpose(MID[:, 8 * b:8 * b + 8], extT[:, b * P:(b + 1) * P], I[0:8, 0:8])
                last.then_inc(S["ext_psum"], 1)

            def finish_block(i, k, f):
                pe.wait_ge(S["blk_copied"], NB * f + 2 * i + k + 1)
                pe.wait_ge(S["fin_used"] if f < 3 else (S["h_row"] if f == 3 else S["xo_ready"]),
                           ONE + (NB * f if f < 3 else (4 * NB if f == 3 else 0)) + 2 * i)
                if f == 3:
                    pe.wait_ge(S["hT_block"], ONE + 5 * NB + 2 * i)
                o = NU[k][:, 0:P]
                if f in (0, 2):
                    last = pe.transpose(o, numblk[:, k, :], I[:])
                elif f == 1:
                    mm(o, numblk[:, k, :], I[:], stop=False)
                    mm(o, blkT[:, k, :], rootW[:], start=False, stop=False)
                    last = mm(o, ones_row[:], brow[:, 0, :], start=False)
                else:
                    mm(o, numblk[:, k, :], I[:], stop=False)
                    mm(o, extblk[:, k, :], WeH8T[f - 3][:], start=False)
                    o2 = NU[k][:, P:2 * P]
                    mm(o2, blkT[:, k, :], Wsk[f - 3][:], stop=False)
                    last = mm(o2, ones_row[:], brow[:, 1 + f - 3, :], start=False)
                last.then_inc(S["fin_psum"], 1)

            def self_loops(j):
                for q in range(13):
                    if q > 1:
                        pe.wait_ge(S["gcn_pre_used"], 13 * j + q - 1)
                    if q == 0:
                        pe.wait_ge(S["staged"], ONE + NB * (3 + j))
                    mm(QXf[q % 2][:, 0:256], (G1T, G2T)[j][:], hT[:, 256 * q:256 * q + 256]).then_inc(S["gcn_pre_psum"], 1)

            def graph_sums(j):
                pe.wait_ge(S["gsum_done"], j + 1)
                mm(MTB[:, 0:1], ones_f[:], small[:, 1:2]).then_inc(S["gsum_psum"], 1)
                pe.wait_ge(S["gsum_ready"], 2 * j + 2)
                mm(MTB[:, 1:2], ones_f[:], small[:, 3:4]).then_inc(S["gsum_psum"], 1)

            norm_tables(0, 0)
            attention(ATT[0])
            transposes_of_extras(0)
            with pe.Fori(0, NPAIR) as i:
                for k in range(2):
                    finish_block(i, k, 0)
            for q in range(13):
                pe.wait_ge(S["deg_sqrt"], max(q, 1))
                mm(QXf[q % 2][:, 0:256], sel_deg[:], extT[:, 256 * q:256 * q + 256]).then_inc(S["deg_psum"], 1)
            norm_tables(1, 1)
            linear(LIN[0], 1)
            with pe.Fori(0, NPAIR) as i:
                for k in range(2):
                    finish_block(i, k, 1)
            norm_tables(2, 2)
            self_loops(0)
            linear(LIN[1], 2)
            graph_sums(0)
            with pe.Fori(0, NPAIR) as i:
                for k in range(2):
                    table_block(i, k, 3, blkT)
            self_loops(1)
            linear(LIN[2], 3)
            graph_sums(1)
            with pe.Fori(0, NPAIR) as i:
                for k in range(2):
                    finish_block(i, k, 2)
            norm_tables(3, 4)
            attention(ATT[1])
            transposes_of_extras(1)
            with pe.Fori(0, NPAIR) as i:
                for k in range(2):
                    finish_block(i, k, 3)
                for k in range(2):
                    transpose_row(i, k, 4, 5)
                for k in range(2):
                    table_block(i, k, 5, blk2)
            attention(ATT[2])
            transposes_of_extras(2)
            with pe.Fori(0, NPAIR) as i:
                for k in range(2):
                    finish_block(i, k, 4)


def kernel(**inputs):
    import numpy as _np
    import concourse.bacc as _bacc
    from concourse import mybir as _mybir
    from concourse.bass_utils import run_bass_kernel_spmd as _run

    nc = _bacc.Bacc("TRN2", target_bir_lowering=False, num_devices=1)
    arrays, args = {}, {}
    for name, value in inputs.items():
        a = _np.ascontiguousarray(value)
        arrays[f"in_{name}_dram"] = a
        args[name] = nc.dram_tensor(f"in_{name}_dram", a.shape, _mybir.dt.from_np(a.dtype), kind="ExternalInput").ap()
    out = nc.dram_tensor("out_0_dram", inputs["x"].shape, _mybir.dt.float32, kind="ExternalOutput").ap()
    gnn_stack_kernel(nc, args, out)
    r = _run(nc, [arrays], core_ids=[0])
    return r.results[0]["out_0_dram"]
```

```python
import concourse.bass as bass
from concourse import mybir
from contextlib import ExitStack


class Tally:

    def __init__(self, sem):
        self.sem, self.n, self.at = sem, 0, None

    def enter(self, i, per):
        self.at = (i, per, self.n)

    def leave(self, trips):
        _, per, start = self.at
        self.n, self.at = start + per * trips, None

    def leave_iteration(self):
        assert self.n - self.at[2] == self.at[1], (self.n - self.at[2], self.at[1])

    def step(self, instruction):
        instruction.then_inc(self.sem, 1)
        self.n += 1
        return self.value()

    def value(self):
        return self.n if self.at is None else self.at[0] * self.at[1] + self.n


def gnn_stack_kernel(nc, A, out):
    f32, bf16, i32, u32 = mybir.dt.float32, mybir.dt.bfloat16, mybir.dt.int32, mybir.dt.uint32
    ALU, ACT, AX = mybir.AluOpType, mybir.ActivationFunctionType, mybir.AxisListType
    ds = bass.ds

    N, D = A["x"].shape
    E = A["src"].shape[0]
    P = 128
    TPG, GPC = 4, 8
    TPC = TPG * GPC
    NCH = -(-E // (P * TPC))
    T = NCH * TPC
    EP = T * P
    NB = 2 * -(-(N + P) // (2 * P))
    NP = NB * P
    NPAIR = NB // 2
    NG = NCH * GPC
    SPAN = TPG * P
    R1, R2, R3 = (P * t + 1 for t in range(1, TPG))
    assert TPG == 4 and R1 * R2 * R3 < 1 << 24
    QS = 2
    FREE = GPC
    ONE = 8
    HEADS, HD = 4, D // 4
    NREL, NBASE = A["L1_gnn_w_comp"].shape
    BIG = 1e30
    EPS = 1e-5
    LASTROWS = N - (N // P) * P
    FULLB = N // P
    assert NP % NCH == 0 and NCH * TPC * P - E < P and TPC * HEADS == P

    ctx = ExitStack()
    with ctx:
        ctx.enter_context(nc.allow_non_contiguous_dma(reason="columns of a few vectors, and one value for each window"))

        def sb(name, shape, dt=f32):
            return ctx.enter_context(nc.sbuf_tensor(name, shape, dt))

        def sem(name):
            return ctx.enter_context(nc.semaphore(name))

        def dram(name, shape, dt=f32):
            return nc.dram_tensor(name, shape, dt).ap()

        dpad = dram("dst_padded", (EP + 2,), i32)
        drow = dram("dst_in_window", (EP,), bf16)
        penrow_d = dram("open_tiles", (2, NCH, TPC), bf16)
        att0_d = dram("gat_rows", (NP, 132))
        rel_d = dram("relation_rows", (NP * NREL, D))
        gcn_d = dram("gcn_rows", (NP, D))
        kv_d = dram("key_value_rows", (NP, 2 * D))
        q0_d = dram("gat_target_scores", (NP, 4))
        q_d = dram("query_rows", (NP, 132))

        xN = sb("x_rows", [P, NB, D])
        hT = sb("h_transposed", [P, NP])
        numS = sb("sums_transposed", [P, N + SPAN])
        extS = sb("extra_sums_transposed", [8, N + SPAN])
        numT, extT = numS[:, 0:NP], extS[:, 0:NP]
        ring = sb("gathered_rows", [P, TPC * 2 * D])
        vbuf = sb("kept_values", [P, TPC * 132])
        ident = sb("identity", [P, P])
        iota_j = sb("iota_window", [P, P])
        zeros_w = sb("zero_weights", [P, P], bf16)
        neg_iota_p = sb("minus_partition", [P, 1])
        ones_row = sb("ones_row", [1, P])
        dstP = sb("dst_in_window_by_edge", [P, T])
        startP = sb("segment_start_by_edge", [P, T])
        ewP = sb("edge_weight_by_edge", [P, T])
        srcI = sb("src_index", [P, T + TPC], i32)
        relI = sb("src_relation_index", [P, T + TPC], i32)
        idx_slot = sb("index_slot", [P, TPC], i32)
        fpen = sb("start_penalty", [P, NCH, P], bf16)
        bpen = sb("end_penalty_reversed", [P, NCH, P], bf16)
        prefF = sb("start_seen_penalty", [P, NCH, P], bf16)
        prefB = sb("end_ahead_penalty", [P, NCH, P], bf16)
        penF_row = sb("tile_penalty_forward", [1, NCH, HEADS, TPC + 1], bf16)
        penB_row = sb("tile_penalty_backward_reversed", [1, NCH, HEADS, TPC], bf16)
        cont_row = sb("chunk_continues", [1, NCH])
        baseI = sb("window_base", [1, NCH * TPC], i32)
        span_baseI = sb("group_span_base", [1, NG], i32)
        tile_offI = sb("tile_offsets_in_span", [1, NG], i32)
        nbI = sb("shared_node", [1, NCH], i32)
        Sb = sb("edge_node_onehot", [P, GPC, TPG, P])
        prod = sb("query_key_products", [P, 2, TPG * D])
        msg = sb("messages", [P, 2, TPG, D])
        STa = sb("window_distance", [P, 2, TPG * P], bf16)
        ST = sb("node_edge_onehot", [P, 2, TPG * P])
        drow_sb = sb("dst_in_window_row", [P, 2, (GPC // 2) * TPG * P], bf16)
        qwin = sb("query_window", [P, QS, TPG, 132])
        alpha = sb("scores", [P, HEADS, TPC])
        alphax = sb("scan_scores", [P, HEADS, TPC])
        qwe = sb("query_edge_term", [P, HEADS, TPC])
        am = sb("scores_below_max", [P, HEADS, TPC])
        pe8 = sb("edge_factors", [P, 8, TPC])
        Fs = sb("forward_max", [P, P])
        Bs = sb("backward_max", [P, P])
        Ms = sb("segment_max", [P, P])
        M2s = sb("segment_max_backward", [P, P])
        rin = sb("tile_last_max", [1, HEADS, TPC + 1])
        SF = sb("tile_forward_max", [1, HEADS, TPC + 1])
        before_row = sb("max_before_tile", [1, P])
        after_row = sb("max_after_tile", [1, P])
        delta = sb("max_change", [1, 2, HEADS])
        delta_feat = sb("max_change_by_feature", [1, P])
        delta_ext3 = sb("max_change_by_extra", [1, 8])
        delta_ext0 = sb("max_change_by_gat_extra", [1, 4])
        facs = sb("rescale_factors", [P, 2])
        hrow = sb("normed_block", [P, 2, D])
        blkT = sb("transposed_block", [P, 2, P])
        numblk = sb("sums_block", [P, 2, P])
        rstd = sb("inverse_deviation", [P, NB])
        nbias = sb("minus_mean_scaled", [P, NB])
        eps_t = sb("epsilon", [P, 1])
        dinvN = sb("inverse_root_degree", [P, NB])
        exN = sb("extra_by_node", [P, NB, 8])
        R0 = sb("gat_weights", [P, 132])
        acol = sb("gat_vectors", [P, 2])
        Wr = sb("relation_weights", [P, NREL, D])
        rootW = sb("root_weight", [P, D])
        G1T = sb("gcn_w1_transposed", [P, P])
        G2T = sb("gcn_w2_transposed", [P, P])
        gcol = sb("gcn_columns", [P, 6])
        brow = sb("bias_rows", [1, 3, D])
        Rq = [sb(f"query_key_value_weights_{i}", [P, 388]) for i in range(2)]
        bq = [sb(f"query_key_value_bias_{i}", [1, 388]) for i in range(2)]
        Wsk = [sb(f"skip_weight_{i}", [P, D]) for i in range(2)]
        WeH8 = [sb(f"edge_weight_by_head_{i}", [P, 8]) for i in range(2)]
        WeH8T = [sb(f"edge_weight_by_head_row_{i}", [8, D]) for i in range(2)]
        wecol = sb("edge_weight_columns", [P, 4])
        small = sb("gcn_small", [P, 16])
        pads_sb = sb("pads", [1, 1 + P], i32)
        iota_pi = sb("partition_int", [P, 1], i32)
        ones_f = sb("ones", [P, P])
        headmask = sb("head_mask", [P, HEADS])
        sel_deg = sb("degree_row_selector", [8, P])
        done_mark = sb("done_mark", [1, 1])
        sbrow = sb("tile_backward_row", [1, P])
        wcomp = sb("relation_coefficients", [P, NREL * NBASE])

        ring4 = ring[:].rearrange("p (t w) -> p t w", w=2 * D)
        stage = Sb[:].rearrange("p g t j -> p (g t j)")
        stage2 = [stage[:, 0:1024], stage[:, 1024:2048]]
        hdT = vbuf[:, 0:NP]
        dinvT = ring[:, TPC * D:TPC * D + NP]
        W1nat, W2nat, g1nat, g2nat = (prod[:, 0, m * D:(m + 1) * D] for m in range(4))
        node_work = STa[:].rearrange("p k n -> p (k n)").bitcast(f32)
        stats, mv, exN2 = (node_work[:, NB * a:NB * (a + n)].rearrange("p (b n) -> p b n", n=n)
                           for a, n in ((0, 6), (6, 2), (8, 8)))
        extblk = msg[0:8, 0, 0:2, :]
        tmpA = msg[:, 1, 0:2, :]
        blk2 = prod[:, 0, 0:2 * P].rearrange("p (k n) -> p k n", n=P)
        basisW = prod[:, 1, :].rearrange("p (b d) -> p b d", d=D)
        wqT = ST[:, 0, 0:2 * P].rearrange("p (q d) -> p q d", d=P)
        iota_i = numblk[:, 0, :].bitcast(i32)

        dst3 = [ring[:, j * NCH * P:(j + 1) * NCH * P].rearrange("q (c p) -> q c p", p=P) for j in range(3)]
        base_col = ring[0:TPC, 3 * NCH * P:3 * NCH * P + NCH]
        penB_in = ring[0:1, 3 * NCH * P + P:3 * NCH * P + P + NCH * P // 2].bitcast(bf16).rearrange("q (c h t) -> q c h t", h=HEADS, t=TPC)
        tile_f, span_f, pair_f = (vbuf[0:1, 2 * NCH * P + a:2 * NCH * P + a + n]
                                  for a, n in ((0, T), (T, NG), (T + NG, NG)))
        src_in = vbuf[0:TPC, 0:NCH * P].rearrange("q (c p) -> q c p", p=P)
        type_in = vbuf[0:TPC, NCH * P:2 * NCH * P].rearrange("q (c p) -> q c p", p=P)
        ew_in = numT[0:TPC, 0:NCH * P].rearrange("q (c p) -> q c p", p=P)
        dst_rel = numT[0:TPC, NCH * P:2 * NCH * P].rearrange("q (c p) -> q c p", p=P)
        drow_out = msg[0:TPC].rearrange("p a t d -> p (a t d)").bitcast(bf16)[:, 0:NCH * P].rearrange("q (c p) -> q c p", p=P)
        wx = hT[:].rearrange("p (b d) -> p b d", d=D)

        QX = [ctx.enter_context(nc.psum_tensor(f"QX{i}", [P, TPG, 256], f32)) for i in range(2)]
        NU = [ctx.enter_context(nc.psum_tensor(f"NU{i}", [P, 512], f32)) for i in range(2)]
        MID = ctx.enter_context(nc.psum_tensor("MID", [P, 512], f32))
        MTB = ctx.enter_context(nc.psum_tensor("MTB", [P, 512], f32))
        EX = [MID, MTB]
        QXf = [q[:].rearrange("p t w -> p (t w)") for q in QX]

        names = """spans_ready consts_ready edges_zeroed edges_loaded dst_copied pads_stored dst_loaded x_zeroed x_loaded
            weights_in1  lanes_ready lanesT_ready  drow_stored pen_stored pen_loaded idx_ready
            wT_ready wT_used wmul_ready prep_done src_ready
            dve act_own pool_own
            idx_copied slot_taken k_used v_kept rows_used
            drow_in0 drow_in1 st_ready expand_done prod_done qwe_kept
            alpha_ready xT_ready scans_ready rows_ready rowscan_ready cols_ready M_ready MT_ready am_ready
            delta_ready fac_psum ident_ready wprep_done we_ready r0_ready tab_kept rescaled gsum_done lin_used p_ready fac_ready msg_ready s_ready nu_ready nu_used factors_ready
            zeroed stats_ready sqrt_done norm_ready h_row hT_psum hT_block tab_psum staged stored0 stored1
            gcn_pre_psum gcn_pre_used
            blk_copied fin_psum fin_used ext_psum  deg_psum deg_sqrt   
            gsum_psum gsum_ready gsq_ready gcn_done    out_stored0  xo_ready
            numT_ready  hT_all deg_ready""".split()
        S = {n: sem(n) for n in names}
        gathered = [sem(f"gathered{g}") for g in range(GPC)]
        qwin_in = [sem(f"qwin_in{g}") for g in range(GPC)]
        NDL = 16 * (3 * HEADS + 3)
        STORES = [2, 1, 1, 1, 2, 2]
        NWEIGHTS = 6 + 2 * 10 + 4 + 6
        PER = {False: 8, True: 14}
        SBASE = [0, 4 * NG, 5 * NG, NG, 2 * NG, 3 * NG]
        STB = [16 + 16 * NPAIR * sum(STORES[:n + 1]) for n in range(6)]

        block = ctx.enter_context(nc.Block())

        ATT = [dict(k=0, H=1, table=att0_d, width=132, win=q0_d, ww=4, v0=0),
               dict(k=1, H=HEADS, table=kv_d, width=2 * D, win=q_d, ww=132, v0=D),
               dict(k=2, H=HEADS, table=kv_d, width=2 * D, win=q_d, ww=132, v0=D)]
        LIN = [dict(k=0, table=rel_d, idx=relI), dict(k=1, table=gcn_d, idx=srcI), dict(k=2, table=gcn_d, idx=srcI)]
        ORDER = ["att0", "lin0", "lin1", "lin2", "att1", "att2"]
        att_base = lambda a: a["k"] * NG
        stores_before = lambda n: 16 * NPAIR * (n + 1)

        @block.sync
        def _(sp):
            sp.dma_start(dpad[1:E + 1].rearrange("(a b) -> a b", b=E // 125),
                         A["dst"].rearrange("(a b) -> a b", b=E // 125)).then_inc(S["dst_copied"], 16)
            sp.wait_ge(S["x_zeroed"], 1)
            sp.dma_start(xN[:, 0:FULLB, :], A["x"][0:FULLB * P, :].rearrange("(b p) d -> p b d", p=P)
                         ).then_inc(S["x_loaded"], 16)
            sp.dma_start(xN[0:LASTROWS, FULLB, :], A["x"][FULLB * P:N, :]).then_inc(S["x_loaded"], 16)
            full = (NCH - 1) * TPC * P
            rows = (E - full) // P
            sp.wait_ge(S["edges_zeroed"], 1)
            for name, to in (("src", src_in.bitcast(i32)), ("edge_type_8", type_in.bitcast(i32)), ("edge_weight", ew_in)):
                sp.dma_start(to[:, 0:NCH - 1, :], A[name][0:full].rearrange("(c t p) -> t c p", t=TPC, p=P)
                             ).then_inc(S["edges_loaded"], 16)
                sp.dma_start(to[0:rows, NCH - 1, :], A[name][full:full + rows * P].rearrange("(t p) -> t p", p=P)
                             ).then_inc(S["edges_loaded"], 16)
                sp.dma_start(to[rows:rows + 1, NCH - 1, 0:E - full - rows * P],
                             A[name][full + rows * P:E].unsqueeze(0)).then_inc(S["edges_loaded"], 16)
            sp.wait_ge(S["dst_copied"], 16)
            sp.wait_ge(S["pads_stored"], 32)
            for j in range(3):
                v = dpad[j:j + EP].rearrange("(c t p) -> t c p", t=TPC, p=P)
                for h in range(HEADS):
                    sp.dma_start(dst3[j].bitcast(i32)[TPC * h:TPC * h + TPC], v).then_inc(S["dst_loaded"], 16)
            bv = dpad[1:EP + 1].rearrange("(c t p) -> t c p", t=TPC, p=P)
            sp.dma_start(base_col.bitcast(i32), bv[:, :, 0]).then_inc(S["dst_loaded"], 16)
            sp.dma_start(baseI[:], dpad[1:EP + 1].rearrange("(g q) -> g q", q=P)[:, 0].unsqueeze(0)).then_inc(S["dst_loaded"], 16)
            sp.dma_start(nbI[:], dpad[0:EP].rearrange("(c q) -> c q", q=TPC * P)[:, 0].unsqueeze(0)).then_inc(S["dst_loaded"], 16)
            sp.wait_ge(S["lanes_ready"], 1)
            sp.dma_start(drow.rearrange("(c t p) -> t c p", t=TPC, p=P), drow_out).then_inc(S["stored0"], 16)
            sp.wait_ge(S["lanes_ready"], 2)
            sp.dma_start(penrow_d[0].rearrange("c t -> t c"), prefF[0:TPC, :, P - 1]).then_inc(S["stored1"], 16)
            sp.dma_start(penrow_d[1].rearrange("c t -> t c"), prefB[0:TPC, :, 0]).then_inc(S["pen_stored"], 16)
            sp.wait_ge(S["pen_stored"], 16)
            sp.wait_ge(S["stored1"], 16)
            for h in range(HEADS):
                sp.dma_start(penF_row[:, :, h, 1:TPC + 1], penrow_d[0:1]).then_inc(S["pen_loaded"], 16)
                sp.dma_start(penB_in[:, :, h, 0:TPC - 1], penrow_d[1:2, :, 0:TPC - 1]).then_inc(S["pen_loaded"], 16)

            def store_tables(n, parts):
                with sp.Fori(0, NPAIR) as i:
                    for k in range(2):
                        sp.wait_ge(S["staged"], ONE + 2 * NPAIR * n + 2 * i + k + 1)
                        for m, (table, width, off) in enumerate(parts):
                            ins = sp.dma_start(table[ds((2 * i + k) * P, P), :], stage2[k][:, off:off + width])
                            ins.then_inc(S[f"stored{k}"], 16)

            def attention_inputs(a):
                b = att_base(a)
                with sp.Fori(0, NCH) as c:
                    for g in range(GPC):
                        if g % (GPC // 2) == 0:
                            half = g // (GPC // 2)
                            sp.wait_ge(S["st_ready"], ONE + b + GPC * c)
                            sp.dma_start(drow_sb[:, half, :], drow[ds(c * TPC * P + half * TPC * P // 2, TPC * P // 2)]
                                         .unsqueeze(0).broadcast_to([P, TPC * P // 2])).then_inc(S[f"drow_in{half}"], 16)
                        bases = [sp.value_load(baseI[0:1, ds(c * TPC + TPG * g + t, 1)], min_val=0, max_val=N) for t in range(TPG)]
                        sp.wait_ge(S["expand_done"], ONE + b + GPC * c + g - QS + 1)
                        for t in range(TPG):
                            sp.dma_start(qwin[:, g % QS, t, 0:a["ww"]], a["win"][ds(bases[t], P), :]).then_inc(qwin_in[g], 16)

            store_tables(0, [(att0_d, 132, 0), (q0_d, 4, 129)])
            sp.wait_ge(S["stored0"], STB[0])
            sp.wait_ge(S["stored1"], STB[0])
            attention_inputs(ATT[0])
            store_tables(1, [(rel_d.rearrange("(n r) d -> n (r d)", r=NREL), NREL * D, 0)])
            store_tables(2, [(gcn_d, D, 0)])
            store_tables(3, [(gcn_d, D, 0)])
            for n, a in ((4, ATT[1]), (5, ATT[2])):
                store_tables(n, [(kv_d, 2 * D, 0), (q_d, 132, 2 * D)])
                sp.wait_ge(S["stored0"], STB[n])
                sp.wait_ge(S["stored1"], STB[n])
                attention_inputs(a)
            sp.wait_ge(S["xo_ready"], ONE + NB)
            sp.dma_start(out[0:FULLB * P, :].rearrange("(b p) d -> p b d", p=P), xN[:, 0:FULLB, :]).then_inc(S["out_stored0"], 16)
            sp.dma_start(out[FULLB * P:N, :], xN[0:LASTROWS, FULLB, :]).then_inc(S["out_stored0"], 16)
            sp.wait_ge(S["out_stored0"], 32)

        @block.gpsimd
        def _(pool):
            own = Tally(S["pool_own"])
            pool.memset(xN[:, FULLB:NB, :], 0.0).then_inc(S["x_zeroed"], 1)
            pool.memset(pads_sb[0:1, 0:1], -1)
            pool.memset(pads_sb[0:1, 1:1 + P], N).then_inc(S["consts_ready"], 1)
            for to in (src_in.bitcast(i32), type_in.bitcast(i32), ew_in):
                last = pool.memset(to[:, NCH - 1, :], 0)
            last.then_inc(S["edges_zeroed"], 1)
            pool.iota(iota_i, [[1, P]], base=0, channel_multiplier=0).then_inc(S["consts_ready"], 1)
            pool.iota(iota_pi[:], [[1, 1]], base=0, channel_multiplier=1).then_inc(S["consts_ready"], 1)
            pool.memset(ones_row[:], 1.0)
            pool.memset(eps_t[:], EPS).then_inc(S["consts_ready"], 1)
            pool.memset(pe8[:], 1.0)
            pool.memset(zeros_w[:], 0.0)
            for q in range(2):
                pool.memset(WeH8[q][:], 0.0)
            pool.memset(penF_row[:], -BIG)
            pool.memset(penB_in, -BIG)
            pool.memset(rin[:], -BIG)
            pool.memset(srcI[:, T:T + TPC], 0)
            pool.memset(relI[:, T:T + TPC], 0)
            pool.memset(alphax[:], 0.0)
            pool.memset(after_row[:], -BIG)
            pool.memset(delta_ext0[:], 0.0)
            pool.memset(extS[:], 0.0).then_inc(S["consts_ready"], 1)

            def gathers(n, table, width, idx, free, base):
                pool.wait_ge(S["stored0"], STB[n])
                pool.wait_ge(S["stored1"], STB[n])
                rows = ring[:, 0:TPC * width].rearrange("p (t w) -> p t w", w=width)
                HG = GPC // 2

                def copy_indices(c, half, done):
                    if half:
                        pool.wait_ge(S[free[-1]], base[-1] + FREE + GPC * c)
                        pool.sem_inc(S["slot_taken"], 1)
                    elif done is not None:
                        for g in range(HG):
                            pool.wait_ge(gathered[g], 16 * TPG * (n * NCH + done))
                            pool.sem_inc(S["slot_taken"], 1)
                    pool.tensor_copy(idx_slot[:, HG * TPG * half:HG * TPG * (half + 1)],
                                     idx[:, ds(c * TPC + HG * TPG * half, HG * TPG)]).then_inc(S["idx_copied"], 1)

                copies = n * (2 * NCH + 1)
                if n:
                    pool.wait_ge(S["idx_copied"], copies)
                copy_indices(0, 0, 0 if n else None)
                with pool.Fori(0, NCH) as c:
                    for g in range(GPC):
                        if g == 3:
                            copy_indices(c, 1, c)
                        if g == 6:
                            copy_indices(c + 1, 0, c + 1)
                        if g % HG == 0:
                            pool.wait_ge(S["idx_copied"], copies + 2 * c + 1 + (g > 0))
                            pool.sem_inc(S["slot_taken"], 1)
                        for s, b in zip(free, base):
                            pool.wait_ge(S[s], b + GPC * c + g + 1)
                            pool.sem_inc(S["slot_taken"], 1)
                        for t in range(TPG * g, TPG * g + TPG):
                            pool.indirect_dma_start(
                                out=rows[:, t, :], out_offset=None, in_=table,
                                in_offset=bass.IndirectOffsetOnAxis(ap=idx_slot[:, t:t + 1].bitcast(u32), axis=0)
                            ).then_inc(gathered[g], 16)

            pool.wait_ge(S["idx_ready"], 2)
            gathers(0, att0_d, 132, srcI, ("v_kept",), (0,))
            gathers(1, rel_d, D, relI, ("rows_used",), (0,))
            gathers(2, gcn_d, D, srcI, ("rows_used",), (NG + FREE,))
            gathers(3, gcn_d, D, srcI, ("rows_used",), (2 * (NG + FREE),))
            gathers(4, kv_d, 2 * D, srcI, ("k_used", "v_kept"), (0, NG + FREE))
            gathers(5, kv_d, 2 * D, srcI, ("k_used", "v_kept"), (NG + FREE, 2 * (NG + FREE)))

        @block.scalar
        def _(act):
            own = Tally(S["act_own"])
            for name in ("st_ready", "staged", "h_row", "qwe_kept"):
                act.sem_inc(S[name], ONE)
            act.wait_ge(S["consts_ready"], 1)
            act.dma_start(dpad[0:1].unsqueeze(0), pads_sb[0:1, 0:1]).then_inc(S["pads_stored"], 16)
            act.dma_start(dpad[E + 1:EP + 2].unsqueeze(0), pads_sb[0:1, 1:EP + 2 - E]).then_inc(S["pads_stored"], 16)

            def load(dst, src):
                act.dma_start(dst, src).then_inc(S["weights_in1"], 16)

            load(W1nat, A["L0_gnn_W1"])
            load(W2nat, A["L0_gnn_W2"])
            load(acol[:, 0:1], A["L0_gnn_a_t"].unsqueeze(1))
            load(acol[:, 1:2], A["L0_gnn_a_s"].unsqueeze(1))
            load(g1nat, A["L2_gnn_W1"])
            load(g2nat, A["L2_gnn_W2"])
            for q in range(2):
                for m, x in enumerate("kvq"):
                    load(Rq[q][:, m * D:(m + 1) * D], A[f"L3_gnn_W{x}{q + 1}"])
                    load(bq[q][:, m * D:(m + 1) * D], A[f"L3_gnn_b{x}{q + 1}"].unsqueeze(0))
                load(Wsk[q][:], A[f"L3_gnn_Ws{q + 1}"])
                load(wecol[:, q:q + 1], A[f"L3_gnn_We{q + 1}"].rearrange("a d -> d a"))
                load(wecol[:, 2 + q:3 + q], A[f"L3_gnn_bq{q + 1}"].unsqueeze(1))
                load(brow[:, 1 + q, :], A[f"L3_gnn_bs{q + 1}"].unsqueeze(0))
            load(basisW, A["L1_gnn_weight"].rearrange("b i o -> i b o"))
            load(wcomp[:], A["L1_gnn_w_comp"].rearrange("r b -> (r b)").unsqueeze(0).broadcast_to([P, NREL * NBASE]))
            load(rootW[:], A["L1_gnn_root_weight"])
            load(brow[:, 0, :], A["L1_gnn_bias"].unsqueeze(0))
            for m, name in enumerate(("b1", "g1", "be1", "b2", "g2", "be2")):
                load(gcol[:, m:m + 1], A[f"L2_gnn_{name}"].unsqueeze(1))

            SC = HD ** -0.5
            act.wait_ge(S["wT_ready"], 1)
            act.copy(R0[:, 0:D], QXf[1][:, 0:D])
            act.copy(R0[:, D:D + 2], QXf[1][:, 3 * D:3 * D + 2]).then_inc(S["r0_ready"], 1)
            act.copy(G1T[:], QXf[1][:, D:2 * D])
            act.copy(G2T[:], QXf[1][:, 2 * D:3 * D])
            act.copy(wqT.rearrange("p a b -> p (a b)"), QXf[1][:, 512:768]).then_inc(S["wT_used"], 1)
            act.wait_ge(S["wmul_ready"], 1)
            for q in range(2):
                act.mul(Rq[q][:, 2 * D:3 * D], Rq[q][:, 2 * D:3 * D], SC)
                act.mul(Rq[q][:, 3 * D:3 * D + 4], QXf[0][:, 512 + 4 * q:516 + 4 * q], SC)
                act.mul(bq[q][:, 2 * D:3 * D], bq[q][:, 2 * D:3 * D], SC)
                act.mul(bq[q][:, 3 * D:3 * D + 4], QXf[0][0:1, 520 + 4 * q:524 + 4 * q], SC)
                act.copy(WeH8T[q][:], QXf[0][0:8, 640 + 128 * q:768 + 128 * q])
            act.copy(facs[:], neg_iota_p[:].broadcast_to([P, 2])).then_inc(S["wprep_done"], 1)

            def deviations(m):
                act.wait_ge(S["stats_ready"], m + 1)
                act.activation(rstd[:], mv[:, :, 1], ACT.Sqrt, bias=eps_t[:]).then_inc(S["sqrt_done"], 1)

            def normed_blocks(i, k, m):
                act.wait_ge(S["hT_psum"], ONE + NB * m + 2 * i + k - 1)
                act.activation(hrow[:, k, :], xN[:, ds(2 * i + k, 1), :].rearrange("p a d -> p (a d)"), ACT.Relu,
                               bias=nbias[:, ds(2 * i + k, 1)], scale=rstd[:, ds(2 * i + k, 1)]).then_inc(S["h_row"], 1)

            def stage_table(i, k, n):
                act.wait_ge(S["tab_psum"], ONE + NB * n + 2 * i + k + 1)
                act.wait_ge(S[f"stored{k}"], (STB[n - 1] if n else 16) + i * (16 * STORES[n]))
                if n == 0:
                    act.copy(stage2[k][:, 0:132], QXf[k][:, 0:132]).then_inc(S["tab_kept"], 1)
                elif n == 1:
                    act.copy(stage2[k][:, 0:NREL * D], QXf[k][:, 0:NREL * D]).then_inc(S["staged"], 1)
                elif n in (2, 3):
                    act.activation(stage2[k][:, 0:D], QXf[k][:, 0:D], ACT.Copy,
                                   scale=dinvN[:, ds(2 * i + k, 1)]).then_inc(S["staged"], 1)
                else:
                    act.copy(stage2[k][:, 0:388], QXf[k][:, 0:388]).then_inc(S["staged"], 1)

            def norm_tables(m, n):
                deviations(m)
                act.wait_ge(S["norm_ready"], m + 1)
                for k in range(2):
                    normed_blocks(0, k, m)
                with act.Fori(0, NPAIR - 1) as i:
                    for k in range(2):
                        normed_blocks(i + 1, k, m)
                        stage_table(i, k, n)
                for k in range(2):
                    stage_table(NPAIR - 1, k, n)

            def attention(a):
                b, cb, H = att_base(a), a["k"] * NCH, a["H"]
                gb = [0, 4, 5][a["k"]] * 16 * TPG * NCH
                width, v0, L3 = a["width"], a["v0"], a["k"] > 0
                vw = 132 if not L3 else D
                rows = ring[:, 0:TPC * width].rearrange("p (t w) -> p t w", w=width)
                vals = vbuf[:, 0:TPC * vw].rearrange("p (t w) -> p t w", w=vw)
                act.sem_inc(S["v_kept"], FREE)

                def targets(c, g):
                    if g % (GPC // 2) == 0:
                        act.wait_ge(S[f"drow_in{g // (GPC // 2)}"], 16 * cb + 16 * (c + 1))
                    q = g % (GPC // 2) * TPG * P
                    act.wait_ge(S["expand_done"], ONE + b + GPC * c + g - 1)
                    own.step(act.activation(STa[:, g % 2, :], drow_sb[:, g // (GPC // 2), q:q + TPG * P], ACT.Square,
                                            bias=neg_iota_p[:]))
                    act.wait_ge(own.sem, own.value())
                    act.activation(ST[:, g % 2, :], STa[:, g % 2, :], ACT.Relu, bias=1.0, scale=-1.0
                                   ).then_inc(S["st_ready"], 1)

                def values(c, g):
                    act.wait_ge(gathered[g], gb + 16 * TPG * (c + 1))
                    if not isinstance(c, int):
                        act.wait_ge(S["msg_ready"], ONE + b + GPC * (c - 1) + g + 1)
                    act.copy(vals[:, TPG * g:TPG * g + TPG, :], rows[:, TPG * g:TPG * g + TPG, v0:v0 + vw]
                             ).then_inc(S["v_kept"], 1)

                def edge_terms(c, g):
                    act.wait_ge(S["k_used"], (a["k"] - 1) * (NG + FREE) + FREE + GPC * c + g + 1)
                    act.wait_ge(S["alpha_ready"], ONE + cb + c)
                    act.copy(qwe[:, :, TPG * g:TPG * (g + 1)].rearrange("p h t -> p t h"),
                             QX[g % 2][:, :, D:D + HEADS]).then_inc(S["qwe_kept"], 1)

                def front(c):
                    for g in range(GPC):
                        if g + 2 < GPC:
                            targets(c, g + 2)
                        values(c, g)
                        if L3 and g:
                            edge_terms(c, g - 1)
                    if L3:
                        edge_terms(c, GPC - 1)

                def exponentials(c):
                    act.wait_ge(S["am_ready"], ONE + cb + c + 1)
                    act.wait_ge(S["nu_ready"], ONE + b + GPC * c)
                    rws = H if L3 else 2
                    act.activation(pe8[:, 0:rws, :], am[:, 0:rws, :], ACT.Exp).then_inc(S["p_ready"], 1)
                    act.wait_ge(S["fac_psum"], cb + c + 1)
                    act.wait_ge(S["rescaled"], ONE + cb + c)
                    act.activation(facs[:, 0:1], MTB[:, P:P + 1], ACT.Exp)
                    ex = 8 if L3 else 3
                    act.activation(facs[0:ex, 1:2], MTB[0:ex, P + 1:P + 2], ACT.Exp).then_inc(S["fac_ready"], 1)

                for g in range(2):
                    targets(0, g)
                front(0)
                with act.Fori(0, NCH - 1) as c:
                    own.enter(c, GPC)
                    for g in range(2):
                        targets(c + 1, g)
                    exponentials(c)
                    front(c + 1)
                    own.leave_iteration()
                own.leave(NCH - 1)
                exponentials(NCH - 1)

            def copy_blocks(i, k, f, src):
                b = ds((2 * i + k) * P, P)
                act.wait_ge(S["fin_psum"], ONE + NB * f + 2 * i + k - 1)
                if f in (1, 3, 4):
                    act.copy(blkT[:, k, :], hT[:, b])
                if f in (3, 4):
                    act.copy(extblk[:, k, :], extT[:, b])
                act.copy(numblk[:, k, :], src[:, b]).then_inc(S["blk_copied"], 1)

            norm_tables(0, 0)
            attention(ATT[0])
            act.wait_ge(S["numT_ready"], 1)
            with act.Fori(0, NPAIR) as i:
                for k in range(2):
                    copy_blocks(i, k, 0, numT)
            act.wait_ge(S["deg_ready"], 1)
            act.activation(dinvN[:], exN[:, :, 2], ACT.Sqrt, bias=1.0).then_inc(S["deg_sqrt"], 1)
            norm_tables(1, 1)
            for j in range(13):
                act.wait_ge(S["deg_psum"], j + 1)
                act.activation(dinvT[:, j * 256:(j + 1) * 256], QXf[j % 2][:, 0:256], ACT.Sqrt, bias=1.0
                               ).then_inc(S["deg_sqrt"], 1)
            act.wait_ge(S["numT_ready"], 2)
            with act.Fori(0, NPAIR) as i:
                for k in range(2):
                    copy_blocks(i, k, 1, numT)
            norm_tables(2, 2)

            def graph_norm(j):
                act.wait_ge(S["numT_ready"], 3 + j)
                act.activation(vbuf[:, 0:N], numT[:, 0:N], ACT.Identity, accum_out=small[:, 0:1]).then_inc(S["gsum_ready"], 1)
                act.wait_ge(S["gsq_ready"], 2 * j + 1)
                act.activation(vbuf[:, 0:N], numT[:, 0:N], ACT.Square, bias=small[:, 2:3], accum_out=small[:, 3:4]
                               ).then_inc(S["gsum_ready"], 1)
                act.wait_ge(S["gsum_psum"], 2 * j + 2)
                act.activation(small[:, 4:5], MTB[:, 1:2], ACT.Sqrt, bias=eps_t[:], scale=1.0 / (N * D)).then_inc(S["sqrt_done"], 1)
                act.wait_ge(S["gsq_ready"], 2 * j + 2)
                act.activation(hT[:], numT[:], ACT.Relu, bias=small[:, 7:8], scale=small[:, 6:7]).then_inc(S["hT_all"], 1)

            graph_norm(0)
            act.wait_ge(S["hT_all"], 1)
            with act.Fori(0, NPAIR) as i:
                for k in range(2):
                    act.wait_ge(S["tab_psum"], ONE + NB * 3 + 2 * i + k - 1)
                    act.copy(blkT[:, k, :], hT[:, ds((2 * i + k) * P, P)]).then_inc(S["hT_block"], 1)
                for k in range(2):
                    stage_table(i, k, 3)
            graph_norm(1)
            act.wait_ge(S["hT_all"], 2)
            with act.Fori(0, NPAIR) as i:
                for k in range(2):
                    copy_blocks(i, k, 2, hT)
            norm_tables(3, 4)
            attention(ATT[1])
            act.wait_ge(S["numT_ready"], 5)
            with act.Fori(0, NPAIR) as i:
                for k in range(2):
                    copy_blocks(i, k, 3, numT)
                for k in range(2):
                    stage_table(i, k, 5)
            attention(ATT[2])
            act.wait_ge(S["numT_ready"], 6)
            with act.Fori(0, NPAIR) as i:
                for k in range(2):
                    copy_blocks(i, k, 4, numT)

        @block.vector
        def _(dve):
            d = Tally(S["dve"])
            for name in ("msg_ready", "alpha_ready", "nu_used", "hT_block", "fin_used", "rescaled", "am_ready", "xo_ready", "lin_used"):
                dve.sem_inc(S[name], ONE)

            def then(ins):
                dve.wait_ge(d.sem, d.step(ins))

            def tt(o, x, y, op):
                return dve.tensor_tensor(o, x, y, op)

            dve.wait_ge(S["consts_ready"], 5)
            dve.tensor_copy(iota_j[:], iota_i)
            then(dve.tensor_copy(small[:, 15:16], iota_pi[:]))
            dve.tensor_scalar(neg_iota_p[:], small[:, 15:16], -1.0, None, ALU.mult)
            dve.tensor_scalar(ident[:], iota_j[:], small[:, 15:16], None, ALU.is_equal).then_inc(S["ident_ready"], 1)
            dve.memset(ones_f[:], 1.0)
            then(dve.memset(headmask[:], 0.0))
            for h in range(HEADS):
                last = dve.memset(headmask[HD * h:HD * (h + 1), h:h + 1], 1.0)
            then(last)
            then(dve.tensor_copy(sel_deg[:], ident[0:8, 2:3].broadcast_to([8, P])))
            dve.wait_ge(S["edges_loaded"], 16 * 9)
            dve.tensor_copy(src_in, src_in.bitcast(i32)).then_inc(S["src_ready"], 1)
            dve.tensor_copy(type_in, type_in.bitcast(i32)).then_inc(S["src_ready"], 1)
            dve.wait_ge(S["weights_in1"], 16 * NWEIGHTS)
            for q in range(2):
                dve.tensor_scalar(WeH8[q][:, 4:8], headmask[:], wecol[:, q:q + 1], None, ALU.mult).then_inc(S["we_ready"], 1)
            dve.wait_ge(S["dst_loaded"], NDL)
            i3 = [x.bitcast(i32) for x in dst3]
            then(tt(dst_rel, i3[1][0:TPC], base_col.bitcast(i32).unsqueeze(2).broadcast_to([TPC, NCH, P]), ALU.subtract))
            dve.tensor_copy(drow_out, dst_rel)
            tt(dst3[0], i3[1], i3[0], ALU.not_equal)
            then(tt(dst3[2], i3[1], i3[2], ALU.not_equal))
            dve.tensor_scalar(nbI[:], nbI[:], 0, None, ALU.max)
            dve.tensor_scalar(cont_row[:], dst3[0][0:1, :, 0], -1.0, 1.0, ALU.mult, ALU.add).then_inc(S["lanes_ready"], 1)
            dve.tensor_scalar(fpen[:], dst3[0], -BIG, None, ALU.mult)
            then(dve.tensor_scalar(bpen[:, :, ::-1], dst3[2], -BIG, None, ALU.mult))
            for c in range(NCH):
                dve.tensor_tensor_scan(prefF[:, c, :], ones_f[:], fpen[:, c, :], 0.0, ALU.mult, ALU.add)
                last = dve.tensor_tensor_scan(prefB[:, c, ::-1], ones_f[:], bpen[:, c, :], 0.0, ALU.mult, ALU.add)
            last.then_inc(S["lanes_ready"], 1)
            then(dve.tensor_copy(tile_f, baseI[:]))
            tf = tile_f.rearrange("q (g t) -> q g t", t=TPG)
            then(dve.tensor_copy(span_f, tf[:, :, 0]))
            then(tt(tf, tf, span_f.unsqueeze(2).broadcast_to([1, NG, TPG]), ALU.subtract))
            dve.tensor_copy(span_baseI[:], span_f)
            then(dve.scalar_tensor_tensor(pair_f, tf[:, :, 3], float(R2), tf[:, :, 2], ALU.mult, ALU.add))
            then(dve.scalar_tensor_tensor(pair_f, pair_f, float(R1), tf[:, :, 1], ALU.mult, ALU.add))
            dve.tensor_copy(tile_offI[:], pair_f).then_inc(S["spans_ready"], 1)
            dve.wait_ge(S["lanesT_ready"], 5)
            then(dve.tensor_copy(srcI[:, 0:T], MID[:, 0:T]))
            dve.scalar_tensor_tensor(relI[:, 0:T], srcI[:, 0:T], float(NREL), MTB[:, 0:T], ALU.mult, ALU.add)
            dve.tensor_copy(ewP[:], QXf[0][:, 0:T])
            dve.tensor_copy(dstP[:], NU[0][:, 0:T])
            dve.tensor_copy(startP[:], NU[1][:, 0:T]).then_inc(S["idx_ready"], 2)
            dve.memset(numS[:], 0.0).then_inc(S["zeroed"], 1)
            for q in range(NBASE):
                for r in range(NREL):
                    co = wcomp[:, NBASE * r + q:NBASE * r + q + 1]
                    if q == 0:
                        last = dve.tensor_scalar(Wr[:, r, :], basisW[:, 0, :], co, None, ALU.mult)
                    else:
                        last = dve.scalar_tensor_tensor(Wr[:, r, :], basisW[:, q, :], co, Wr[:, r, :], ALU.mult, ALU.add)
                then(last)
            dve.wait_ge(S["pen_loaded"], 16 * 2 * HEADS)
            then(dve.tensor_copy(penB_row[:].rearrange("q c h t -> q (c h) t")[:, :, ::-1],
                                 penB_in.rearrange("q c h t -> q (c h) t")))
            dve.wait_ge(S["r0_ready"], 1)
            then(tt(R0[:, 130:131], R0[:, 128:129], R0[:, 129:130], ALU.add))
            dve.tensor_scalar(R0[:, 131:132], R0[:, 130:131], 0.2, None, ALU.mult).then_inc(S["r0_ready"], 1)

            def norm_stats(m):
                for b in range(NB):
                    last = dve.bn_stats(stats[:, b, :], xN[:, b, :])
                then(last)
                for b in range(NB):
                    last = dve.bn_aggr(mv[:, b, :], stats[:, b, :])
                last.then_inc(S["stats_ready"], 1)
                dve.wait_ge(S["sqrt_done"], m + 1 + (2 if m == 3 else 0))
                then(dve.reciprocal(rstd[:], rstd[:]))
                dve.scalar_tensor_tensor(nbias[:], mv[:, :, 0], -1.0, rstd[:], ALU.mult, ALU.mult).then_inc(S["norm_ready"], 1)

            def transposed_block(i, k, m, n, to):
                dve.wait_ge(S["hT_psum"], ONE + NB * m + 2 * i + k + 1)
                if n:
                    dve.tensor_copy(hT[:, ds((2 * i + k) * P, P)], NU[k][:, 256:384])
                dve.wait_ge(S["tab_psum"], ONE + NB * n + 2 * i + k - 1)
                dve.tensor_copy(to[:, k, :], NU[k][:, 256:384]).then_inc(S["hT_block"], 1)

            def norm_tables(m, n):
                norm_stats(m)
                with dve.Fori(0, NPAIR) as i:
                    for k in range(2):
                        transposed_block(i, k, m, n, blkT)
                    if n == 0:
                        for k in range(2):
                            dve.wait_ge(S["tab_kept"], 2 * i + k + 1)
                            dve.tensor_copy(wx[:, ds(2 * i + k, 1), :].rearrange("p a d -> p (a d)"), QXf[k][:, 0:D])
                            tt(stage2[k][:, 132:133], stage2[k][:, 130:131], stage2[k][:, 131:132], ALU.max
                               ).then_inc(S["staged"], 1)

            def span_base(c, g):
                return dve.value_load(span_baseI[0:1, ds(c * GPC + g, 1)], min_val=0, max_val=N)

            def attention(a):
                b, cb, H = att_base(a), a["k"] * NCH, a["H"]
                L3 = a["k"] > 0
                LN = P
                gb = [0, 4, 5][a["k"]] * 16 * TPG * NCH
                kb = (a["k"] - 1) * (NG + FREE) + FREE
                vb = a["k"] * (NG + FREE) + FREE
                vw = 132 if not L3 else D
                ex = 8 if L3 else 3
                vals = vbuf[:, 0:TPC * vw].rearrange("p (t w) -> p t w", w=vw)
                rows = ring4
                for k in range(2):
                    dve.wait_ge(S[f"stored{k}"], STB[(0, 4, 5)[a["k"]]])
                if L3:
                    dve.sem_inc(S["k_used"], FREE)
                then(dve.memset(rin[:], -BIG))
                def products(c, g):
                    dve.wait_ge(S["expand_done"], ONE + b + GPC * c + g + 1)
                    dve.wait_ge(gathered[g], gb + 16 * TPG * (c + 1))
                    if g >= 2:
                        dve.wait_ge(d.sem, d.value())
                    tt(prod[:, g % 2, :].rearrange("p (t w) -> p t w", w=D), QX[g % 2][:, :, 0:D],
                       rows[:, TPG * g:TPG * g + TPG, 0:D], ALU.mult).then_inc(S["k_used"], 1)

                def head_sums(c, g):
                    dve.wait_ge(S["k_used"], kb + GPC * c + g + 1)
                    d.step(dve.tensor_reduce(
                        alphax[:, :, TPG * g:TPG * g + TPG].rearrange("p h t -> p t h"),
                        prod[:, g % 2, :].rearrange("p (t h d) -> p t h d", t=TPG, h=HEADS), AX.X, ALU.add))

                def at(x, c):
                    return x[:, c, :] if isinstance(c, int) else x[:, ds(c, 1), :].rearrange("p a d -> p (a d)")

                def softmax_factors(c, shared, ahead):
                    def onehots(g0, g1):
                        for g in range(g0, g1):
                            tt(Sb[:, g], iota_j[:].unsqueeze(1).broadcast_to([P, TPG, P]),
                               dstP[:, ds(c * TPC + TPG * g, TPG)].unsqueeze(2).broadcast_to([P, TPG, P]),
                               ALU.is_equal).then_inc(S["s_ready"], 1)

                    if L3:
                        dve.wait_ge(S["qwe_kept"], ONE + (a["k"] - 1) * NG + GPC * c + GPC)
                        then(tt(am[:], qwe[:], ewP[:, ds(c * TPC, TPC)].unsqueeze(1).broadcast_to([P, HEADS, TPC]), ALU.mult))
                        tt(alpha[:], am[:], alphax[:], ALU.add).then_inc(S["alpha_ready"], 1)
                        dve.wait_ge(S["alpha_ready"], ONE + cb + c + 1)
                        scan_in = alpha
                    else:
                        dve.wait_ge(S["expand_done"], ONE + b + GPC * c + GPC)
                        dve.wait_ge(S["v_kept"], vb + GPC * c + GPC)
                        qx = QXf[0][:, 0:4 * TPC].rearrange("p (t w) -> p t w", w=4)
                        then(tt(qwe[:, 0, :], vals[:, :, D], qx[:, :, 0], ALU.add))
                        then(dve.scalar_tensor_tensor(alpha[:, 0, :], qwe[:, 0, :], 0.2, qwe[:, 0, :], ALU.mult, ALU.max))
                        tt(alphax[:, 0, :], alpha[:, 0, :], qx[:, :, 3], ALU.max).then_inc(S["alpha_ready"], 1)
                    onehots(0, 2)
                    dve.wait_ge(S["xT_ready"], cb + c + 1)
                    fp = at(fpen, c)
                    bp = at(bpen, c)
                    dve.tensor_tensor_scan(Fs[0:LN, :], fp, MID[0:LN, 0:P], -BIG, ALU.add, ALU.max)
                    dve.tensor_tensor_scan(Bs[0:LN, ::-1], bp, MID[0:LN, P - 1::-1], -BIG, ALU.add, ALU.max
                                           ).then_inc(S["scans_ready"], 1)
                    onehots(2, 4)
                    dve.wait_ge(S["rows_ready"], cb + c + 1)
                    then(dve.tensor_copy(rin[:, :, 1:TPC + 1], MID[0:1, P:P + LN].rearrange("p (h t) -> p h t", h=HEADS)))
                    penF = penF_row[:, ds(c, 1), :, :].rearrange("p a h t -> p (a h t)")
                    penB = penB_row[:, ds(c, 1), :, :].rearrange("p a h t -> p (a h t)")
                    flat = lambda x: x[:, :, :].rearrange("p h t -> p (h t)")
                    then(dve.tensor_tensor_scan(flat(SF), penF, flat(rin), -BIG, ALU.add, ALU.max))
                    byh = lambda x: x[:, 0:LN].rearrange("p (h t) -> p h t", h=HEADS)
                    dve.tensor_copy(byh(before_row), SF[:, :, 0:TPC])
                    sbk = sbrow[:, 0:LN]
                    then(dve.tensor_tensor_scan(sbk[:, ::-1], penB, MID[0:1, 2 * P + LN - 1:2 * P - 1:-1], -BIG,
                                                ALU.add, ALU.max))
                    dve.tensor_copy(byh(after_row)[:, :, 0:TPC - 1], byh(sbrow)[:, :, 1:TPC]).then_inc(S["rowscan_ready"], 1)
                    onehots(4, 6)
                    dve.wait_ge(S["cols_ready"], cb + c + 1)
                    pf = at(prefF, c)
                    pb = at(prefB, c)
                    dve.scalar_tensor_tensor(Ms[0:LN, :], pf, MID[0:LN, 384:385], Fs[0:LN, :], ALU.add, ALU.max)
                    then(dve.scalar_tensor_tensor(M2s[0:LN, :], pb, MID[0:LN, 385:386], Bs[0:LN, :], ALU.add, ALU.max))
                    tt(Ms[0:LN, :], Ms[0:LN, :], M2s[0:LN, :], ALU.max).then_inc(S["M_ready"], 1)
                    onehots(6, 8)
                    dve.wait_ge(S["MT_ready"], cb + c + 1)
                    mt = MTB[:, 0:LN].rearrange("p (h t) -> p h t", h=HEADS)
                    last = tt(am[:, 0:H, :], alpha[:, 0:H, :], mt[:, 0:H, :], ALU.subtract)
                    if not L3:
                        then(dve.tensor_copy(am[:, 2, :], mt[:, 0, :]))
                        last = tt(am[:, 1, :], qx[:, :, 3], am[:, 2, :], ALU.subtract)
                    last.then_inc(S["am_ready"], 1)
                    dl = delta[:, :, 0:H]
                    mnew = MTB[0:1, 0:LN].rearrange("p (h t) -> p h t", h=HEADS)[:, 0:H, 0].unsqueeze(1).broadcast_to([1, 2, H])
                    then(tt(dl, rin[:, 0:H, 0].unsqueeze(1).broadcast_to([1, 2, H]), mnew, ALU.subtract))
                    dve.tensor_scalar(delta_feat[:].rearrange("p (h d) -> p h d", h=H),
                                      dl[:, 0, :].unsqueeze(2).broadcast_to([1, H, D // H]),
                                      cont_row[:, ds(c, 1)], None, ALU.mult)
                    dve.tensor_scalar((delta_ext3 if L3 else delta_ext0)[:, 0:2 * H].rearrange("p (a h) -> p a h", h=H), dl,
                                      cont_row[:, ds(c, 1)], None, ALU.mult).then_inc(S["delta_ready"], 1)
                    dve.tensor_copy(rin[:, 0:HEADS, 0:1], SF[:, 0:HEADS, TPC:TPC + 1])
                    if ahead and L3:
                        products(c + 1, 0)
                    dve.wait_ge(S["fac_ready"], cb + c + 1)
                    dve.wait_ge(S["nu_used"], ONE + b + GPC * c)
                    dve.tensor_scalar(numT[:, ds(shared, 1)], numT[:, ds(shared, 1)], facs[:, 0:1], None, ALU.mult)
                    dve.tensor_scalar(extT[0:ex, ds(shared, 1)], extT[0:ex, ds(shared, 1)], facs[0:ex, 1:2], None, ALU.mult
                                      ).then_inc(S["rescaled"], 1)
                    dve.wait_ge(S["p_ready"], cb + c + 1)
                    if L3:
                        tt(pe8[:, HEADS:2 * HEADS, :], pe8[:, 0:HEADS, :],
                           ewP[:, ds(c * TPC, TPC)].unsqueeze(1).broadcast_to([P, HEADS, TPC]), ALU.mult).then_inc(S["factors_ready"], 1)
                    else:
                        tt(pe8[:, 1, :], pe8[:, 1, :], startP[:, ds(c * TPC, TPC)], ALU.mult).then_inc(S["factors_ready"], 1)
                    dve.wait_ge(S["rescaled"], ONE + cb + c + 1)


                def add_sums(c, g, base):
                    dve.wait_ge(S["nu_ready"], ONE + b + GPC * c + g + 1)
                    dve.wait_ge(S["nu_used"], ONE + b + GPC * c + g)
                    w = ds(base, SPAN)
                    tt(numS[:, w], numS[:, w], NU[g % 2][:], ALU.add)
                    tt(extS[0:ex, w], extS[0:ex, w], EX[g % 2][0:ex, 0:SPAN], ALU.add).then_inc(S["nu_used"], 1)

                def messages(c, g):
                    dve.wait_ge(S["v_kept"], vb + GPC * c + g + 1)
                    dve.wait_ge(S["nu_ready"], ONE + b + GPC * c + max(g - 1, 0))
                    v = vals[:, TPG * g:TPG * g + TPG, 0:D].rearrange("p t (h d) -> p t h d", h=H)
                    f = pe8[:, 0:H, TPG * g:TPG * g + TPG].rearrange("p h t -> p t h").unsqueeze(3).broadcast_to([P, TPG, H, D // H])
                    tt(msg[:, g % 2].rearrange("p t (h d) -> p t h d", h=H), v, f, ALU.mult).then_inc(S["msg_ready"], 1)

                def chunk(c, ahead):
                    shared = dve.value_load(nbI[0:1, ds(c, 1)], min_val=0, max_val=N)
                    softmax_factors(c, shared, ahead)
                    messages(c, 0)
                    for g in range(GPC):
                        base = span_base(c, g - 1) if g else None
                        if g:
                            add_sums(c, g - 1, base)
                        if g + 1 < GPC:
                            messages(c, g + 1)
                        if ahead and L3 and g:
                            products(c + 1, g)
                            head_sums(c + 1, g - 1)
                    if ahead and L3:
                        head_sums(c + 1, GPC - 1)
                    add_sums(c, GPC - 1, span_base(c, GPC - 1))

                if L3:
                    for g in range(GPC):
                        products(0, g)
                        if g:
                            head_sums(0, g - 1)
                    head_sums(0, GPC - 1)
                with dve.Fori(0, NCH - 1) as c:
                    d.enter(c, PER[L3])
                    chunk(c, True)
                    d.leave_iteration()
                d.leave(NCH - 1)
                chunk(NCH - 1, False)
                dve.wait_ge(S["nu_used"], ONE + b + NG)

            def linear(p):
                b = p["k"] * NG
                for k in range(2):
                    dve.wait_ge(S[f"stored{k}"], STB[1 + p["k"]])
                with dve.Fori(0, NCH) as c:
                    for g in range(GPC):
                        if g == 0:
                            dve.wait_ge(S["rows_used"], p["k"] * (NG + FREE) + FREE + GPC * c)
                        tt(Sb[:, g], iota_j[:].unsqueeze(1).broadcast_to([P, TPG, P]),
                           dstP[:, ds(c * TPC + TPG * g, TPG)].unsqueeze(2).broadcast_to([P, TPG, P]),
                           ALU.is_equal).then_inc(S["s_ready"], 1)
                    for g in range(GPC):
                        base = span_base(c, g)
                        dve.wait_ge(S["rows_used"], p["k"] * (NG + FREE) + FREE + GPC * c + g + 1)
                        dve.wait_ge(S["lin_used"], ONE + b + GPC * c + g)
                        w = ds(base, SPAN)
                        tt(numS[:, w], numS[:, w], NU[g % 2][:], ALU.add).then_inc(S["lin_used"], 1)
                    if p["k"] == 0:
                        dve.wait_ge(S["deg_sqrt"], 14)
                        piece = dinvT[:, ds(c * (NP // NCH), NP // NCH)]
                        dve.reciprocal(piece, piece)
                dve.wait_ge(S["lin_used"], ONE + b + NG)

            def extras():
                dve.wait_ge(S["ext_psum"], EXT[0] + 1)
                EXT[0] += 1
                then(dve.tensor_copy(exN[:].rearrange("p b e -> p (b e)"), MID[:, 0:8 * NB]))

            EXT = [0]
            dve.wait_ge(S["x_loaded"], 32)
            norm_tables(0, 0)
            attention(ATT[0])
            dve.memset(done_mark[:], 0.0).then_inc(S["numT_ready"], 1)
            extras()
            dve.memset(done_mark[:], 0.0).then_inc(S["deg_ready"], 1)
            then(dve.tensor_scalar(exN2[:, :, 0], exN[:, :, 0], 0.0, None, ALU.is_equal))
            then(tt(exN2[:, :, 1], exN[:, :, 1], exN2[:, :, 0], ALU.add))
            then(tt(exN2[:, :, 2], exN[:, :, 0], exN2[:, :, 1], ALU.add))
            then(dve.reciprocal(exN2[:, :, 3], exN2[:, :, 2]))
            with dve.Fori(0, NPAIR) as i:
                d.enter(i, 2)
                for k in range(2):
                    b = ds(2 * i + k, 1)
                    dve.wait_ge(S["fin_psum"], ONE + 2 * i + k + 1)
                    dve.scalar_tensor_tensor(tmpA[:, k, :], wx[:, b, :].rearrange("p a d -> p (a d)"), exN2[:, b, 1], NU[k][:, 0:P],
                                             ALU.mult, ALU.add).then_inc(S["fin_used"], 1)
                    dve.wait_ge(S["fin_used"], ONE + 2 * i + k + 1)
                    xb = xN[:, b, :].rearrange("p a d -> p (a d)")
                    d.step(dve.scalar_tensor_tensor(xb, tmpA[:, k, :], exN2[:, b, 3], xb, ALU.mult, ALU.add))
                d.leave_iteration()
            d.leave(NPAIR)
            dve.wait_ge(d.sem, d.value())
            dve.wait_ge(S["deg_sqrt"], 1)
            then(dve.reciprocal(dinvN[:], dinvN[:]))
            dve.memset(numS[:], 0.0)
            dve.memset(done_mark[:], 0.0).then_inc(S["zeroed"], 1)
            norm_tables(1, 1)
            linear(LIN[0])
            dve.memset(done_mark[:], 0.0).then_inc(S["numT_ready"], 1)
            with dve.Fori(0, NPAIR) as i:
                for k in range(2):
                    xb = xN[:, ds(2 * i + k, 1), :].rearrange("p a d -> p (a d)")
                    dve.wait_ge(S["fin_psum"], ONE + NB + 2 * i + k + 1)
                    dve.scalar_tensor_tensor(xb, NU[k][:, 0:P], 0.0, xb, ALU.max, ALU.add).then_inc(S["fin_used"], 1)
            dve.wait_ge(S["fin_used"], ONE + 2 * NB)
            then(dve.memset(numS[:], 0.0))
            norm_tables(2, 2)

            def graph_layer(j):
                for q in range(13):
                    dve.wait_ge(S["gcn_pre_psum"], 13 * j + q + 1)
                    w = slice(256 * q, 256 * q + 256)
                    tt(hdT[:, w], QXf[q % 2][:, 0:256], dinvT[:, w], ALU.mult).then_inc(S["gcn_pre_used"], 1)
                linear(LIN[1 + j])
                then(tt(numT[:], numT[:], hdT, ALU.add))
                tt(numT[:], numT[:], dinvT, ALU.mult).then_inc(S["numT_ready"], 1)
                dve.wait_ge(S["gsum_ready"], 2 * j + 1)
                bc, gc, bec = (gcol[:, 3 * j + m:3 * j + m + 1] for m in range(3))
                dve.scalar_tensor_tensor(small[:, 1:2], bc, float(N), small[:, 0:1], ALU.mult, ALU.add
                                         ).then_inc(S["gsum_done"], 1)
                dve.wait_ge(S["gsum_psum"], 2 * j + 1)
                dve.scalar_tensor_tensor(small[:, 2:3], MTB[:, 0:1], -1.0 / (N * D), bc, ALU.mult, ALU.add).then_inc(S["gsq_ready"], 1)
                dve.wait_ge(S["sqrt_done"], 3 + j + 1)
                then(dve.reciprocal(small[:, 5:6], small[:, 4:5]))
                then(tt(small[:, 6:7], small[:, 5:6], gc, ALU.mult))
                dve.scalar_tensor_tensor(small[:, 7:8], small[:, 2:3], small[:, 6:7], bec, ALU.mult, ALU.add
                                         ).then_inc(S["gsq_ready"], 1)
                dve.wait_ge(S["hT_all"], j + 1)
                then(dve.memset(numS[:], 0.0))

            graph_layer(0)
            graph_layer(1)
            with dve.Fori(0, NPAIR) as i:
                for k in range(2):
                    xb = xN[:, ds(2 * i + k, 1), :].rearrange("p a d -> p (a d)")
                    dve.wait_ge(S["fin_psum"], ONE + 2 * NB + 2 * i + k + 1)
                    tt(xb, NU[k][:, 0:P], xb, ALU.add).then_inc(S["fin_used"], 1)
            dve.wait_ge(S["fin_used"], ONE + 3 * NB)
            then(dve.memset(extS[:], 0.0))
            norm_tables(3, 4)
            for j in range(2):
                attention(ATT[1 + j])
                dve.memset(done_mark[:], 0.0).then_inc(S["numT_ready"], 1)
                extras()
                then(dve.tensor_scalar(exN2[:, :, 0:4], exN[:, :, 0:4], 1e-30, None, ALU.max))
                then(dve.reciprocal(exN2[:, :, 4:8], exN2[:, :, 0:4]))
                with dve.Fori(0, NPAIR) as i:
                    d.enter(i, 2 + 2 * j)
                    for k in range(2):
                        b = ds(2 * i + k, 1)
                        dve.wait_ge(S["fin_psum"], ONE + (3 + j) * NB + 2 * i + k + 1)
                        rden = exN2[:, b, 4:8].rearrange("p a h -> p (a h)").unsqueeze(2).broadcast_to([P, HEADS, HD])
                        then(tt(tmpA[:, k, :].rearrange("p (h d) -> p h d", h=HEADS),
                                NU[k][:, 0:P].rearrange("p (h d) -> p h d", h=HEADS), rden, ALU.mult))
                        if j == 0:
                            dve.wait_ge(S["hT_psum"], ONE + 4 * NB + 2 * i + k - 1)
                            tt(hrow[:, k, :], tmpA[:, k, :], NU[k][:, P:2 * P], ALU.add).then_inc(S["h_row"], 1)
                        else:
                            then(tt(tmpA[:, k, :], tmpA[:, k, :], NU[k][:, P:2 * P], ALU.add))
                            xb = xN[:, b, :].rearrange("p a d -> p (a d)")
                            tt(xb, tmpA[:, k, :], xb, ALU.add).then_inc(S["xo_ready"], 1)
                    d.leave_iteration()
                    for k in range(2 if j == 0 else 0):
                        transposed_block(i, k, 4, 5, blk2)
                d.leave(NPAIR)
                if j == 0:
                    dve.wait_ge(S["fin_psum"], ONE + 4 * NB)
                    dve.memset(numS[:], 0.0)
                    then(dve.memset(extS[:], 0.0))

        @block.tensor
        def _(pe):
            I = ident
            for name in ("expand_done", "nu_ready", "hT_psum", "tab_psum", "fin_psum"):
                pe.sem_inc(S[name], ONE)

            def mm(o, l, r, start=True, stop=True):
                return pe.matmul(o, l, r, start=start, stop=stop)

            pe.wait_ge(S["ident_ready"], 1)
            pe.wait_ge(S["src_ready"], 2)
            for x, to in ((src_in, MID[:]), (type_in, MTB[:]), (ew_in, QXf[0])):
                for c in range(NCH):
                    last = pe.transpose(to[:, TPC * c:TPC * (c + 1)], x[:, c, :], I[0:TPC, 0:TPC])
                last.then_inc(S["lanesT_ready"], 1)
            pe.wait_ge(S["weights_in1"], 16 * NWEIGHTS)
            pe.transpose(QXf[1][:, 0:D], W1nat, I[:])
            pe.transpose(QXf[1][:, D:2 * D], g1nat, I[:])
            pe.transpose(QXf[1][:, 2 * D:3 * D], g2nat, I[:])
            mm(QXf[1][:, 3 * D:3 * D + 1], W1nat, acol[:, 0:1])
            mm(QXf[1][:, 3 * D + 1:3 * D + 2], W2nat, acol[:, 1:2])
            for q in range(2):
                last = pe.transpose(QXf[1][:, 512 + D * q:512 + D * (q + 1)], Rq[q][:, 2 * D:3 * D], I[:])
            last.then_inc(S["wT_ready"], 1)
            pe.wait_ge(S["lanes_ready"], 1)
            for x, to in ((dst_rel, NU[0][:]), (dst3[0][0:TPC], NU[1][:])):
                for c in range(NCH):
                    last = pe.transpose(to[:, TPC * c:TPC * (c + 1)], x[:, c, :], I[0:TPC, 0:TPC])
                last.then_inc(S["lanesT_ready"], 1)
            pe.wait_ge(S["wT_used"], 1)
            pe.wait_ge(S["we_ready"], 2)
            for q in range(2):
                mm(QXf[0][:, 512 + 4 * q:516 + 4 * q], wqT[:, q, :], WeH8[q][:, 4:8])
                mm(QXf[0][0:1, 520 + 4 * q:524 + 4 * q], wecol[:, 2 + q:3 + q], WeH8[q][:, 4:8])
                last = pe.transpose(QXf[0][0:8, 640 + 128 * q:768 + 128 * q], WeH8[q][:], I[:])
            last.then_inc(S["wmul_ready"], 1)
            pe.wait_ge(S["wprep_done"], 1)
            pe.wait_ge(S["idx_ready"], 2)
            pe.wait_ge(S["r0_ready"], 2)

            def transpose_row(i, k, m, n):
                pe.wait_ge(S["h_row"], ONE + NB * m + 2 * i + k + 1)
                pe.wait_ge(S["hT_block"], ONE + NB * n + 2 * i + k - 1)
                pe.transpose(NU[k][:, 256:384], hrow[:, k, :], I[:]).then_inc(S["hT_psum"], 1)

            def table_block(i, k, n, block):
                pe.wait_ge(S["hT_block"], ONE + NB * n + 2 * i + k + 1)
                pe.wait_ge(S["staged"], ONE + NB * n + 2 * i + k - 1)
                h = block[:, k, :]
                if n == 0:
                    last = mm(QXf[k][:, 0:132], h, R0[:])
                elif n == 1:
                    w = Wr[:].rearrange("p r d -> p (r d)")
                    mm(QXf[k][:, 0:512], h, w[:, 0:512])
                    last = mm(QXf[k][:, 512:1024], h, w[:, 512:1024])
                elif n in (2, 3):
                    last = mm(QXf[k][:, 0:D], h, (G1T, G2T)[n - 2][:])
                else:
                    mm(QXf[k][:, 0:388], h, Rq[n - 4][:], stop=False)
                    last = mm(QXf[k][:, 0:388], ones_row[:], bq[n - 4][:], start=False)
                last.then_inc(S["tab_psum"], 1)

            def norm_tables(m, n):
                for k in range(2):
                    transpose_row(0, k, m, n)
                with pe.Fori(0, NPAIR - 1) as i:
                    for k in range(2):
                        table_block(i, k, n, blkT)
                        transpose_row(i + 1, k, m, n)
                for k in range(2):
                    table_block(NPAIR - 1, k, n, blkT)

            pe.wait_ge(S["spans_ready"], 1)

            def offsets(c, g):
                v = pe.value_load(tile_offI[0:1, ds(c * GPC + g, 1)], min_val=0, max_val=R1 * R2 * R3 - 1)
                v2 = v // R1
                return [0, v % R1, v2 % R2, v2 // R2]

            def clear(bank, rows):
                mm(bank[0:rows, 0:SPAN], zeros_w[:, 0:rows],
                   fpen[:, 0:TPG, :].rearrange("q c p -> q (c p)"), True, False)

            def attention(a):
                b, cb, H = att_base(a), a["k"] * NCH, a["H"]
                L3 = a["k"] > 0
                LN = P
                ex = 8 if L3 else 3
                kb = (a["k"] - 1) * (NG + FREE) + FREE
                sb0 = SBASE[a["k"]]

                def expand(c, g):
                    pe.wait_ge(S["st_ready"], ONE + b + GPC * c + g + 1)
                    pe.wait_ge(qwin_in[g], 16 * TPG * cb + 16 * TPG * (c + 1))
                    if L3:
                        pe.wait_ge(S["k_used"], kb + GPC * c + max(g - 1, 0))
                        pe.wait_ge(S["qwe_kept"], ONE + (a["k"] - 1) * NG + GPC * c + max(g - 1, 0))
                    elif g == 0:
                        pe.wait_ge(S["am_ready"], ONE + cb + c)
                    for t in range(TPG):
                        to = QX[g % 2][:, t, 0:132] if L3 else QXf[0][:, 4 * (TPG * g + t):4 * (TPG * g + t) + 4]
                        last = mm(to, ST[:, g % 2, t * P:(t + 1) * P], qwin[:, g % QS, t, 0:a["ww"]])
                    last.then_inc(S["expand_done"], 1)

                def softmax_moves(c, ahead):
                    pe.wait_ge(S["alpha_ready"], ONE + cb + c + 1)
                    x = (alpha if L3 else alphax)[:].rearrange("p h t -> p (h t)")
                    pe.transpose(MID[:, 0:P], x, I[:]).then_inc(S["xT_ready"], 1)
                    pe.wait_ge(S["scans_ready"], cb + c + 1)
                    mm(MID[0:1, P:2 * P], Fs[:, P - 1:P], I[:])
                    mm(MID[0:1, 2 * P:3 * P], Bs[:, 0:1], I[:]).then_inc(S["rows_ready"], 1)
                    pe.wait_ge(S["rowscan_ready"], cb + c + 1)
                    mm(MID[:, 384:385], before_row[:], ones_row[:, 0:1])
                    mm(MID[:, 385:386], after_row[:], ones_row[:, 0:1]).then_inc(S["cols_ready"], 1)
                    pe.wait_ge(S["M_ready"], cb + c + 1)
                    pe.transpose(MTB[:, 0:P], Ms[:], I[:]).then_inc(S["MT_ready"], 1)
                    if ahead and L3:
                        expand(c + 1, 0)
                    pe.wait_ge(S["delta_ready"], cb + c + 1)
                    mm(MTB[:, P:P + 1], delta_feat[:], ones_row[:, 0:1])
                    mm(MTB[0:ex, P + 1:P + 2], (delta_ext3 if L3 else delta_ext0)[:, 0:ex], ones_row[:, 0:1]
                       ).then_inc(S["fac_psum"], 1)
                    pe.wait_ge(S["factors_ready"], cb + c + 1)

                def window_sums(c, g):
                    off = offsets(c, g)
                    pe.wait_ge(S["s_ready"], sb0 + GPC * c + g + 1)
                    pe.wait_ge(S["nu_used"], ONE + b + GPC * c + max(g - 1, 0))
                    clear(EX[g % 2], 8)
                    for t in range(TPG):
                        mm(EX[g % 2][0:ex, ds(off[t], P)], pe8[:, 0:ex, TPG * g + t], Sb[:, g, t, :], False, t == TPG - 1)
                    clear(NU[g % 2], P)
                    pe.wait_ge(S["msg_ready"], ONE + b + GPC * c + g + 1)
                    for t in range(TPG):
                        last = mm(NU[g % 2][:, ds(off[t], P)], msg[:, g % 2, t, :], Sb[:, g, t, :], False, t == TPG - 1)
                    last.then_inc(S["nu_ready"], 1)

                for g in range(GPC):
                    expand(0, g)
                with pe.Fori(0, NCH - 1) as c:
                    softmax_moves(c, True)
                    if not L3:
                        expand(c + 1, 0)
                    for g in range(GPC):
                        if g + 1 < GPC:
                            expand(c + 1, g + 1)
                        window_sums(c, g)
                softmax_moves(NCH - 1, False)
                for g in range(GPC):
                    window_sums(NCH - 1, g)

            def linear(p, n):
                b, sb0 = p["k"] * NG, SBASE[3 + p["k"]]
                rows = ring[:, 0:TPC * D].rearrange("p (t w) -> p t w", w=D)
                pe.sem_inc(S["rows_used"], FREE)
                with pe.Fori(0, NCH) as c:
                    for g in range(GPC):
                        off = offsets(c, g)
                        pe.wait_ge(gathered[g], n * 16 * TPG * NCH + 16 * TPG * (c + 1))
                        pe.wait_ge(S["s_ready"], sb0 + GPC * c + g + 1)
                        pe.wait_ge(S["lin_used"], ONE + b + GPC * c + max(g - 1, 0))
                        clear(NU[g % 2], P)
                        for t in range(TPG):
                            last = mm(NU[g % 2][:, ds(off[t], P)], rows[:, TPG * g + t, :], Sb[:, g, t, :], False, t == TPG - 1)
                        last.then_inc(S["rows_used"], 1)

            def transposes_of_extras(j):
                pe.wait_ge(S["numT_ready"], (1, 5, 6)[j])
                for b in range(NB):
                    last = pe.transpose(MID[:, 8 * b:8 * b + 8], extT[:, b * P:(b + 1) * P], I[0:8, 0:8])
                last.then_inc(S["ext_psum"], 1)

            def finish_block(i, k, f):
                pe.wait_ge(S["blk_copied"], NB * f + 2 * i + k + 1)
                pe.wait_ge(S["fin_used"] if f < 3 else (S["h_row"] if f == 3 else S["xo_ready"]),
                           ONE + (NB * f if f < 3 else (4 * NB if f == 3 else 0)) + 2 * i + k - 1)
                if f == 3:
                    pe.wait_ge(S["hT_block"], ONE + 5 * NB + 2 * i + k - 1)
                o = NU[k][:, 0:P]
                if f in (0, 2):
                    last = pe.transpose(o, numblk[:, k, :], I[:])
                elif f == 1:
                    mm(o, numblk[:, k, :], I[:], stop=False)
                    mm(o, blkT[:, k, :], rootW[:], start=False, stop=False)
                    last = mm(o, ones_row[:], brow[:, 0, :], start=False)
                else:
                    mm(o, numblk[:, k, :], I[:], stop=False)
                    mm(o, extblk[:, k, :], WeH8T[f - 3][:], start=False)
                    o2 = NU[k][:, P:2 * P]
                    mm(o2, blkT[:, k, :], Wsk[f - 3][:], stop=False)
                    last = mm(o2, ones_row[:], brow[:, 1 + f - 3, :], start=False)
                last.then_inc(S["fin_psum"], 1)

            def self_loops(j):
                for q in range(13):
                    if q > 1:
                        pe.wait_ge(S["gcn_pre_used"], 13 * j + q - 1)
                    if q == 0:
                        pe.wait_ge(S["staged"], ONE + NB * (3 + j))
                    mm(QXf[q % 2][:, 0:256], (G1T, G2T)[j][:], hT[:, 256 * q:256 * q + 256]).then_inc(S["gcn_pre_psum"], 1)

            def graph_sums(j):
                pe.wait_ge(S["gsum_done"], j + 1)
                mm(MTB[:, 0:1], ones_f[:], small[:, 1:2]).then_inc(S["gsum_psum"], 1)
                pe.wait_ge(S["gsum_ready"], 2 * j + 2)
                mm(MTB[:, 1:2], ones_f[:], small[:, 3:4]).then_inc(S["gsum_psum"], 1)

            norm_tables(0, 0)
            attention(ATT[0])
            transposes_of_extras(0)
            with pe.Fori(0, NPAIR) as i:
                for k in range(2):
                    finish_block(i, k, 0)
            norm_tables(1, 1)
            pe.wait_ge(S["staged"], ONE + NB * 2)
            for q in range(13):
                pe.wait_ge(S["deg_sqrt"], max(q, 1))
                mm(QXf[q % 2][:, 0:256], sel_deg[:], extT[:, 256 * q:256 * q + 256]).then_inc(S["deg_psum"], 1)
            linear(LIN[0], 1)
            with pe.Fori(0, NPAIR) as i:
                for k in range(2):
                    finish_block(i, k, 1)
            norm_tables(2, 2)
            self_loops(0)
            linear(LIN[1], 2)
            graph_sums(0)
            with pe.Fori(0, NPAIR) as i:
                for k in range(2):
                    table_block(i, k, 3, blkT)
            self_loops(1)
            linear(LIN[2], 3)
            graph_sums(1)
            with pe.Fori(0, NPAIR) as i:
                for k in range(2):
                    finish_block(i, k, 2)
            norm_tables(3, 4)
            attention(ATT[1])
            transposes_of_extras(1)
            with pe.Fori(0, NPAIR) as i:
                for k in range(2):
                    finish_block(i, k, 3)
                for k in range(2):
                    transpose_row(i, k, 4, 5)
                for k in range(2):
                    table_block(i, k, 5, blk2)
            attention(ATT[2])
            transposes_of_extras(2)
            with pe.Fori(0, NPAIR) as i:
                for k in range(2):
                    finish_block(i, k, 4)


def kernel(**inputs):
    import numpy as _np
    import concourse.bacc as _bacc
    from concourse import mybir as _mybir
    from concourse.bass_utils import run_bass_kernel_spmd as _run

    nc = _bacc.Bacc("TRN2", target_bir_lowering=False, num_devices=1)
    arrays, args = {}, {}
    for name, value in inputs.items():
        a = _np.ascontiguousarray(value)
        arrays[f"in_{name}_dram"] = a
        args[name] = nc.dram_tensor(f"in_{name}_dram", a.shape, _mybir.dt.from_np(a.dtype), kind="ExternalInput").ap()
    out = nc.dram_tensor("out_0_dram", inputs["x"].shape, _mybir.dt.float32, kind="ExternalOutput").ap()
    gnn_stack_kernel(nc, args, out)
    r = _run(nc, [arrays], core_ids=[0])
    return r.results[0]["out_0_dram"]
```
